# Optimizing a Trainium2 kernel written in Bass

```python
import numpy as np
import jax
import jax.numpy as jnp

def _softmax(x, axis=-1):
    return jax.nn.softmax(x, axis=axis)

def _gelu(x):
    return jax.nn.gelu(x, approximate=True)

def _silu(x):
    return jax.nn.silu(x)

def _sigmoid(x):
    return jax.nn.sigmoid(x)

def _layernorm(x, axis=-1, eps=1e-05):
    m = jnp.mean(x, axis=axis, keepdims=True)
    v = jnp.var(x, axis=axis, keepdims=True)
    return (x - m) / jnp.sqrt(v + eps)

def _scatter_add(tgt, idx, src, axis=0):
    return tgt.at[idx].add(src)

def _segment_sum(src, seg, n):
    return jax.ops.segment_sum(src, seg, n)
kernel_name = 'mk_gnn_preln_d4_gnn_r16_819a9d'

def setup_inputs(seed: int=0):
    np.random.seed(seed)
    _w = jnp.asarray

    def _rec_inputs():
        import jax
        import jax.numpy as jnp
        _gk = jax.random.key(seed)
        x = -0.0001006 + 1 * jax.random.normal(jax.random.fold_in(_gk, 1), (6250, 96), jnp.float32)
        src = jax.random.randint(jax.random.fold_in(_gk, 2), (100000,), 0, 6250, jnp.int32)
        dst = jnp.minimum((6250 * jax.random.uniform(jax.random.fold_in(_gk, 3), (100000,)) ** 2.0).astype(jnp.int32), 99999)
        _o = jnp.argsort(dst, stable=True)
        src = src[_o]
        dst = dst[_o]
        edge_attr_32 = 0.000196303 + 1.00016 * jax.random.normal(jax.random.fold_in(_gk, 12), (100000, 32), jnp.float32)
        edge_type_8 = jax.random.randint(jax.random.fold_in(_gk, 14), (100000,), 0, 8, jnp.int32)
        return (x, src, dst, edge_attr_32, edge_type_8)
    x, src, dst, edge_attr_32, edge_type_8 = _rec_inputs()

    def _L0_gnn_setup():
        import jax, jax.numpy as jnp
        import numpy as np
        N_NODES = 3125
        N_EDGES = 50000
        IN_DIM = 96
        OUT_DIM = 96
        EDGE_DIM = 32
        BN_EPS = 1e-05
        key = jax.random.key(seed)
        ks = jax.random.split(key, 12)
        x = jax.random.normal(ks[0], (N_NODES, IN_DIM), dtype=jnp.float32)
        edge_index = jax.random.randint(ks[1], (2, N_EDGES), 0, N_NODES, dtype=jnp.int64)
        edge_attr = jax.random.normal(ks[2], (N_EDGES, EDGE_DIM), dtype=jnp.float32)
        We = jax.random.normal(ks[3], (EDGE_DIM, IN_DIM), dtype=jnp.float32) / np.sqrt(EDGE_DIM)
        be = jnp.zeros((IN_DIM,), dtype=jnp.float32)
        W1 = jax.random.normal(ks[4], (IN_DIM, OUT_DIM), dtype=jnp.float32) / np.sqrt(IN_DIM)
        b1 = jnp.zeros((OUT_DIM,), dtype=jnp.float32)
        W2 = jax.random.normal(ks[5], (OUT_DIM, OUT_DIM), dtype=jnp.float32) / np.sqrt(OUT_DIM)
        b2 = jnp.zeros((OUT_DIM,), dtype=jnp.float32)
        gamma = jnp.ones((OUT_DIM,), dtype=jnp.float32)
        beta = jnp.zeros((OUT_DIM,), dtype=jnp.float32)
        return {'x': x, 'edge_index': edge_index, 'edge_attr': edge_attr, 'We': We, 'be': be, 'W1': W1, 'b1': b1, 'W2': W2, 'b2': b2, 'gamma': gamma, 'beta': beta}
    _L0_gnn_all = _L0_gnn_setup()
    _L0_gnn_in = {k: v for k, v in _L0_gnn_all.items() if k in ('We', 'be', 'W1', 'b1', 'W2', 'b2', 'gamma', 'beta')}
    del _L0_gnn_all

    def _L1_gnn_setup():
        import jax, jax.numpy as jnp
        import numpy as np
        N_NODES = 3125

        def gcn_conv(x, src, dst, W, b, n):
            ones = jnp.ones(src.shape[0], dtype=x.dtype)
            deg = jax.ops.segment_sum(ones, dst, num_segments=n) + jnp.asarray(1.0, x.dtype)
            dinv = jax.lax.rsqrt(deg)
            h = x @ W
            norm = dinv[src] * dinv[dst]
            msg = h[src] * norm[:, None]
            out = jax.ops.segment_sum(msg, dst, num_segments=n)
            out = out + h * (dinv * dinv)[:, None] + b
            return out
        key = jax.random.key(seed)
        ks = jax.random.split(key, 9)
        C, D_T = (96, 384)
        E = 50000
        x = jax.random.normal(ks[0], (N_NODES, C), dtype=jnp.float32)
        edge_index = jax.random.randint(ks[1], (2, E), 0, N_NODES, dtype=jnp.int64)
        t_emb = jax.random.normal(ks[2], (1, D_T), dtype=jnp.float32)
        s = 1.0 / np.sqrt(C)
        W1 = jax.random.uniform(ks[3], (C, C), jnp.float32, -s, s)
        b1 = jnp.zeros((C,), jnp.float32)
        W2 = jax.random.uniform(ks[4], (C, C), jnp.float32, -s, s)
        b2 = jnp.zeros((C,), jnp.float32)
        st = 1.0 / np.sqrt(D_T)
        We = jax.random.uniform(ks[5], (D_T, C), jnp.float32, -st, st)
        be = jax.random.uniform(ks[6], (C,), jnp.float32, -st, st)
        return {'x': x, 'edge_index': edge_index, 't_emb': t_emb, 'W1': W1, 'b1': b1, 'W2': W2, 'b2': b2, 'We': We, 'be': be}
    _L1_gnn_all = _L1_gnn_setup()
    _L1_gnn_in = {k: v for k, v in _L1_gnn_all.items() if k in ('t_emb', 'W1', 'b1', 'W2', 'b2', 'We', 'be')}
    del _L1_gnn_all

    def _L2_gnn_setup():
        import jax, jax.numpy as jnp
        import numpy as np
        N_NODES = 3125
        N_EDGES = 50000
        H_DIM = 96
        N_RELS = 8
        N_BASES = 8
        SUBMAT = H_DIM // N_BASES
        N_LAYERS = 2
        key = jax.random.key(seed)
        k1, k2, k3, k4, k5, k6 = jax.random.split(key, 6)
        h = jax.random.normal(k1, (N_NODES, H_DIM), dtype=jnp.float32)
        weights = jax.random.normal(k2, (N_LAYERS, N_RELS, N_BASES, SUBMAT, SUBMAT), dtype=jnp.float32) * 0.1
        loop_w = jax.random.normal(k3, (N_LAYERS, H_DIM, H_DIM), dtype=jnp.float32) * 0.1
        bias = jnp.zeros((N_LAYERS, H_DIM), dtype=jnp.float32)
        src = jax.random.randint(k4, (N_EDGES,), 0, N_NODES, dtype=jnp.int64)
        dst = jax.random.randint(k5, (N_EDGES,), 0, N_NODES, dtype=jnp.int64)
        etype = jax.random.randint(k6, (N_EDGES,), 0, N_RELS, dtype=jnp.int64)
        return {'h': h, 'weights': weights, 'loop_w': loop_w, 'bias': bias, 'src': src, 'dst': dst, 'etype': etype}
    _L2_gnn_all = _L2_gnn_setup()
    _L2_gnn_in = {k: v for k, v in _L2_gnn_all.items() if k in ('weights', 'loop_w', 'bias')}
    del _L2_gnn_all

    def _L3_gnn_setup():
        import jax, jax.numpy as jnp
        import numpy as np
        K = 10
        ALPHA = 0.1
        BETA = 0.9
        N_NODES = 3125
        N_EDGES = 50000
        D_FEAT = 96
        key = jax.random.key(seed)
        k1, k2, k3 = jax.random.split(key, 3)
        x = jax.random.normal(k1, (N_NODES, D_FEAT), dtype=jnp.float32)
        row = jax.random.randint(k2, (N_EDGES,), 0, N_NODES, dtype=jnp.int64)
        col = jax.random.randint(k3, (N_EDGES,), 0, N_NODES, dtype=jnp.int64)
        edge_index = jnp.stack([row, col], axis=0)
        return {'x': x, 'edge_index': edge_index}
    _L3_gnn_all = _L3_gnn_setup()
    _L3_gnn_in = {k: v for k, v in _L3_gnn_all.items() if k in ()}
    del _L3_gnn_all
    return {'x': x, 'src': src, 'dst': dst, 'edge_attr_32': edge_attr_32, 'edge_type_8': edge_type_8, 'L0_gnn_We': _L0_gnn_in['We'], 'L0_gnn_be': _L0_gnn_in['be'], 'L0_gnn_W1': _L0_gnn_in['W1'], 'L0_gnn_b1': _L0_gnn_in['b1'], 'L0_gnn_W2': _L0_gnn_in['W2'], 'L0_gnn_b2': _L0_gnn_in['b2'], 'L0_gnn_gamma': _L0_gnn_in['gamma'], 'L0_gnn_beta': _L0_gnn_in['beta'], 'L1_gnn_t_emb': _L1_gnn_in['t_emb'], 'L1_gnn_W1': _L1_gnn_in['W1'], 'L1_gnn_b1': _L1_gnn_in['b1'], 'L1_gnn_W2': _L1_gnn_in['W2'], 'L1_gnn_b2': _L1_gnn_in['b2'], 'L1_gnn_We': _L1_gnn_in['We'], 'L1_gnn_be': _L1_gnn_in['be'], 'L2_gnn_weights': _L2_gnn_in['weights'], 'L2_gnn_loop_w': _L2_gnn_in['loop_w'], 'L2_gnn_bias': _L2_gnn_in['bias']}

def reference(x, src, dst, edge_attr_32, edge_type_8, L0_gnn_We, L0_gnn_be, L0_gnn_W1, L0_gnn_b1, L0_gnn_W2, L0_gnn_b2, L0_gnn_gamma, L0_gnn_beta, L1_gnn_t_emb, L1_gnn_W1, L1_gnn_b1, L1_gnn_W2, L1_gnn_b2, L1_gnn_We, L1_gnn_be, L2_gnn_weights, L2_gnn_loop_w, L2_gnn_bias):
    import jax
    import jax.numpy as jnp

    def _L0_gnn_ref(x, edge_index, edge_attr, We, be, W1, b1, W2, b2, gamma, beta):
        import jax, jax.numpy as jnp
        import numpy as np
        N_NODES = 3125
        N_EDGES = 50000
        IN_DIM = 96
        OUT_DIM = 96
        EDGE_DIM = 32
        BN_EPS = 1e-05
        src = edge_index[0]
        dst = edge_index[1]
        msg = jax.nn.relu(x[src] + edge_attr @ We + be)
        aggr = jax.ops.segment_sum(msg, dst, num_segments=x.shape[0])
        h = x + aggr
        h = jax.nn.relu(h @ W1 + b1) @ W2 + b2
        mean = jnp.mean(h, axis=0)
        var = jnp.mean(jnp.square(h - mean), axis=0)
        h = (h - mean) * jax.lax.rsqrt(var + BN_EPS) * gamma + beta
        return jax.nn.relu(h)

    def _L1_gnn_ref(x, edge_index, t_emb, W1, b1, W2, b2, We, be):
        import jax, jax.numpy as jnp
        import numpy as np
        N_NODES = 3125

        def gcn_conv(x, src, dst, W, b, n):
            ones = jnp.ones(src.shape[0], dtype=x.dtype)
            deg = jax.ops.segment_sum(ones, dst, num_segments=n) + jnp.asarray(1.0, x.dtype)
            dinv = jax.lax.rsqrt(deg)
            h = x @ W
            norm = dinv[src] * dinv[dst]
            msg = h[src] * norm[:, None]
            out = jax.ops.segment_sum(msg, dst, num_segments=n)
            out = out + h * (dinv * dinv)[:, None] + b
            return out
        src, dst = (edge_index[0], edge_index[1])
        n = x.shape[0]
        h = gcn_conv(x, src, dst, W1, b1, n)
        h = h + jax.nn.silu(t_emb @ We + be)
        h = jax.nn.silu(gcn_conv(h, src, dst, W2, b2, n))
        return x + h

    def _L2_gnn_ref(h, weights, loop_w, bias, src, dst, etype):
        import jax, jax.numpy as jnp
        import numpy as np
        N_NODES = 3125
        N_EDGES = 50000
        H_DIM = 96
        N_RELS = 8
        N_BASES = 8
        SUBMAT = H_DIM // N_BASES
        N_LAYERS = 2
        N, D = h.shape
        L, R, B, S, _ = weights.shape
        E = src.shape[0]
        in_deg = jax.ops.segment_sum(jnp.ones((E,), dtype=h.dtype), dst, num_segments=N)
        node_norm = jnp.where(in_deg > 0, 1.0 / jnp.maximum(in_deg, 1.0), 0.0)
        edge_norm = node_norm[dst][:, None]
        for l in range(L):
            xb = h.reshape(N, B, S)
            transformed = jnp.einsum('nbi,rbio->rnbo', xb, weights[l]).reshape(R, N, D)
            msg = transformed[etype, src] * edge_norm
            agg = jax.ops.segment_sum(msg, dst, num_segments=N)
            h_new = agg + h @ loop_w[l] + bias[l]
            h = jax.nn.relu(h_new) if l < L - 1 else h_new
        return h

    def _L3_gnn_ref(x, edge_index):
        import jax, jax.numpy as jnp
        import numpy as np
        K = 10
        ALPHA = 0.1
        BETA = 0.9
        N_NODES = 3125
        N_EDGES = 50000
        D_FEAT = 96
        n = x.shape[0]
        row, col = (edge_index[0], edge_index[1])
        ones = jnp.ones((edge_index.shape[1],), dtype=x.dtype)
        deg_row = jnp.maximum(jax.ops.segment_sum(ones, row, num_segments=n), 1.0)
        deg_col = jnp.maximum(jax.ops.segment_sum(ones, col, num_segments=n), 1.0)
        w = jax.lax.rsqrt(deg_row[row] * deg_col[col])

        def spmm(feat):
            msg = feat[col] * w[:, None]
            return jax.ops.segment_sum(msg, row, num_segments=n)
        h = x
        out = h
        for _ in range(K):
            out = spmm(out) * BETA + h * ALPHA
        theta = BETA ** K + ALPHA * sum((BETA ** i for i in range(K)))
        return out / jnp.asarray(theta, dtype=x.dtype)
    edge_index = jnp.stack([src, dst])
    h = jnp.maximum(_layernorm(x, axis=-1), 0.0)
    x = x + _L0_gnn_ref(h, edge_index, edge_attr_32, L0_gnn_We, L0_gnn_be, L0_gnn_W1, L0_gnn_b1, L0_gnn_W2, L0_gnn_b2, L0_gnn_gamma, L0_gnn_beta)
    h = jnp.maximum(_layernorm(x, axis=-1), 0.0)
    x = x + _L1_gnn_ref(h, edge_index, L1_gnn_t_emb, L1_gnn_W1, L1_gnn_b1, L1_gnn_W2, L1_gnn_b2, L1_gnn_We, L1_gnn_be)
    h = jnp.maximum(_layernorm(x, axis=-1), 0.0)
    x = x + _L2_gnn_ref(h, L2_gnn_weights, L2_gnn_loop_w, L2_gnn_bias, src, dst, edge_type_8)
    h = jnp.maximum(_layernorm(x, axis=-1), 0.0)
    x = x + _L3_gnn_ref(h, edge_index)
    return x

_drawn_inputs = setup_inputs


def setup_inputs(seed=0):
    import zlib

    import numpy as np

    out = dict(_drawn_inputs(seed))
    spreads = {'L0_gnn_be': (0.0, 0.1),
     'L0_gnn_b1': (0.0, 2.0),
     'L0_gnn_b2': (0.0, 2.0),
     'L0_gnn_gamma': (1.0, 0.2),
     'L0_gnn_beta': (0.0, 0.1),
     'L1_gnn_b1': (0.0, 0.365),
     'L1_gnn_b2': (0.0, 0.1),
     'L2_gnn_bias': (0.0, 0.1)}
    factors = {'L1_gnn_be': 8.0}
    for name, (base, spread) in spreads.items():
        noise = np.random.default_rng([zlib.crc32(name.encode()), seed]).standard_normal(out[name].shape)
        drawn = base * np.exp(spread * noise) if base else spread * noise
        out[name] = jnp.asarray(drawn.astype(out[name].dtype))
    for name, factor in factors.items():
        out[name] = (out[name] * factor).astype(out[name].dtype)
    return out
```

```python
import concourse.bass as bass
from concourse import mybir
from contextlib import ExitStack

F32, I32 = mybir.dt.float32, mybir.dt.int32
ALU, ACT = mybir.AluOpType, mybir.ActivationFunctionType
X = mybir.AxisListType.X
RAN = (mybir.EngineType.DVE,)

P = 128
N, D, E = 6250, 96, 100000
NB = -(-N // P)
LAST = N - (NB - 1) * P
W = NB * D
ED = 32
RELS, BASES = 8, 8
SUB = D // BASES
T_DIM = 384
STEPS = 10
ALPHA, BETA = 0.1, 0.9
THETA = BETA ** STEPS + ALPHA * sum(BETA ** i for i in range(STEPS))

EC = E // P
ER = E - EC * P
ECP = EC + 1
CH = 71
NCH = EC // CH
assert NCH * CH == EC and NCH % 2 == 1

GT = 8
SLOTS = 4
T = 832
assert T >= E // P + NB and T % (GT * SLOTS) == 0
ROUNDS = T // (GT * SLOTS)
GROUPS = T // GT
RW = 36
SW = 2
BANK = 512
CB = BANK // D
NQ = -(-NB // CB)
NT = -(-NB // 4)
HC = 11
HS = EC // HC
assert HS * HC == EC and HS % 2 == 1
CONSTS = 8
WEIGHTS = 4 + 2 * (BASES + 2) + 4 + 4 + 4 + 2

class Count:

    def __init__(self, sem):
        self.sem, self.value, self.kept = sem, 0, []

    def step(self, instruction):
        instruction.then_inc(self.sem, 1)
        self.value = self.value + 1

    def enter(self, i, per):
        self.kept.append((self.value, per))
        self.value = self.value + i * per
        self.at = self.value

    def leave(self, trips):
        before, per = self.kept.pop()
        self.value = before + per * trips

def build(nc, x, src, dst, edge_attr_32, edge_type_8, L0_gnn_We, L0_gnn_be, L0_gnn_W1, L0_gnn_b1,
          L0_gnn_W2, L0_gnn_b2, L0_gnn_gamma, L0_gnn_beta, L1_gnn_t_emb, L1_gnn_W1, L1_gnn_b1,
          L1_gnn_W2, L1_gnn_b2, L1_gnn_We, L1_gnn_be, L2_gnn_weights, L2_gnn_loop_w, L2_gnn_bias, out):
    ctx = ExitStack()
    with ctx:
        ctx.enter_context(nc.allow_non_contiguous_dma("small weights, transposed on the way"))

        def sb(name, shape, dt=F32):
            return ctx.enter_context(nc.sbuf_tensor(name, shape, dt))

        def sem(name):
            return ctx.enter_context(nc.semaphore(name))

        rec_dst = nc.dram_tensor("rec_dst", (P * T, RW), I32).ap()
        rec_src = nc.dram_tensor("rec_src", (P * T, SW), I32).ap()
        table = nc.dram_tensor("node_table", (P * NB, D), F32).ap()
        table_rel = nc.dram_tensor("relation_table", (P * NB * RELS, D), F32).ap()
        table_rows = table.rearrange("(p b) f -> p (b f)", p=P)
        table_rel_rows = table_rel.rearrange("(p b r) f -> p b (r f)", p=P, b=NB)
        rec_dst_rows = rec_dst.rearrange("(p t) w -> p (t w)", p=P)
        rec_src_rows = rec_src.rearrange("(p t) w -> p (t w)", p=P)

        xs = sb("x_residual", [P, W])
        h = sb("h", [P, W])
        acc = sb("edge_sums", [P, W])
        tab = sb("own_term", [P, W])
        hT_whole = sb("h_transposed", [P, NB * P])
        hT = hT_whole[0:D, :]

        tile_rows = sb("table_rows_of_tiles", [P, 2 * T], I32)
        row_src, row_rel = tile_rows[:, 0:T], tile_rows[:, T:2 * T]
        by_src = tile_rows[:, :].rearrange("p (t w) -> p t w", w=SW)
        loc_dst = sb("place_of_target", [P, T])
        off_dst = sb("block_offset_dst", [1, T], I32)
        off_src = sb("block_offset_src", [1, T], I32)
        pos_dst = sb("record_row_dst", [P, ECP], I32)
        pos_src = sb("record_row_src", [P, ECP], I32)
        srow, rrow, dloc = tile_rows[:, 0:ECP], tile_rows[:, ECP:2 * ECP], loc_dst[:, 0:ECP]
        drow = sb("edge_target_row", [P, ECP], I32)
        sloc = sb("edge_source_place", [P, ECP])

        def work(k, dt=F32):
            whole, k = (tab, k) if k < 6 else (hT_whole, k)
            lo = k * ECP if k < 6 else 2 * CH * ED + (k - 6) * ECP
            v = whole[:, lo:lo + ECP]
            return v.bitcast(dt) if dt != F32 else v
        assert 6 * ECP <= W and 2 * CH * ED + 2 * ECP <= NB * P
        ints = {"src": work(0, I32), "dst": work(1, I32), "type": work(2, I32)}
        blk = {"src": work(3), "dst": work(4)}
        cum, eq, pos_f = work(5), work(6, I32), work(7)
        zero_row = acc[:, 0:ECP]
        ea_in = hT_whole[:, 0:2 * CH * ED].rearrange("p (s w) -> p s w", s=2)

        rows = sb("rows", [P, SLOTS, GT * D])
        flat = rows[:, :, :].rearrange("p s w -> p (s w)")
        low, high = flat[:, 0:ECP].bitcast(I32), flat[:, ECP:2 * ECP].bitcast(I32)
        onehot = sb("onehot", [P, 2, GT * P])
        idx_st = sb("staged_rows", [P, SLOTS, GT], I32)
        rec_in = sb("records_in", [P, SLOTS, GT, RW], I32)
        stage = sb("staged_records", [P, 2, CH, RW], I32)
        stage_pos = sb("staged_record_rows", [P, 2, CH], I32)
        ea_flat = sb("edge_features_packed", [P, GT * ED])
        eaT = sb("edge_features_T", [P, P])
        rel_st = stage[:, 0, 0:2 * RELS * D // RW + 1, :].rearrange("p c w -> p (c w)")[:, 0:2 * RELS * D].bitcast(F32).rearrange("p (s w) -> p s w", s=2)

        ident = sb("ident", [P, P])
        ones = sb("ones", [P, P])
        before = sb("before", [P, P])
        upto = sb("upto", [NB, NB])
        places = sb("places", [P, GT * P])
        tile_no = flat[0:NB, 2 * ECP:2 * ECP + T]
        tile_ge = rec_in[0:NB, :, :, :].rearrange("p s t w -> p (s t w)")[:, 0:T].bitcast(F32)
        we_diag = sb("We_diag", [P, 4 * D])
        w1a = sb("L0_W1", [D, D])
        w2a = sb("L0_W2", [D, D])
        w1b = sb("L1_W1", [D, D])
        w2b = sb("L1_W2", [D, D])
        cols = sb("L0_columns", [D, 4])
        rw = [sb(f"relation_W{i}", [D, RELS * D]) for i in range(2)]
        lw = [sb(f"loop_W{i}", [D, D]) for i in range(2)]
        bias2 = sb("L2_bias", [P, 2, D])
        be_row = sb("be_row", [P, D])
        b1_row = sb("L1_b1_row", [P, D])
        b2_row = sb("L1_b2_row", [P, D])
        be1_row = sb("L1_be_row", [P, D])
        t_rep = sb("t_emb_rep", [P, 3, P])
        t_col = sb("t_emb_col", [P, 3])
        we1 = sb("L1_We", [P, 3, D])
        t_row = sb("t_row", [P, D])
        t_sig = sb("t_sig", [P, D])
        cnt = sb("cnt", [P, NB])
        tot = sb("tot", [P, NB])
        tot_i = sb("tot_i", [P, NB], I32)
        ends = sb("ends", [P, NB])
        start = sb("start", [P, NB])
        totT = sb("totT", [NB, 1])
        totT_i = sb("totT_i", [NB, 1], I32)
        endT = sb("endT", [NB, 1])
        deg = {"dst": sb("deg_dst", [P, NB]), "src": sb("deg_src", [P, NB])}
        factors = sb("node_factors", [P, 3, NB])
        dinv, w_row, w_col = factors[:, 0, :], factors[:, 1, :], factors[:, 2, :]
        norm2 = sb("node_norm", [P, NB])
        stats = sb("stats", [P, NB, 6])
        mv = sb("mean_var", [P, NB, 2])
        rstd = sb("rstd", [P, NB])
        bstats = sb("bstats", [D, NT, 6])
        bmv = sb("bmv", [D, 2])
        bcol = sb("bcol", [D, 4])
        hist_room = onehot[:, :, :].rearrange("p s w -> p (s w)").bitcast(mybir.dt.bfloat16)
        oh_loc = hist_room[:, 0:2 * HC * P].rearrange("p (s c n) -> p s c n", s=2, c=HC)
        oh_blk = hist_room[:, 2 * HC * P:2 * HC * (P + NB)].rearrange("p (s c b) -> p s c b", s=2, c=HC)
        blk_no = flat[:, 2 * ECP + T:2 * ECP + T + HC * NB]

        banks = [ctx.enter_context(nc.psum_tensor(f"bank{i}", [P, BANK], F32)) for i in range(8)]
        tbank, pbank, part = banks[0:2], banks[2:4], banks[4:8]

        consts = sem("consts")
        edges_in = sem("edges_in")
        x_in = sem("x_in")
        weights_in = sem("weights_in")
        memset_done = sem("memset_done")
        rec_zero = sem("rec_zero")
        dve_step = sem("dve_step")
        cnt_ready = sem("cnt_ready")
        tot_ready = sem("tot_ready")
        tilesT_ready = sem("tilesT_ready")
        endT_ready = sem("endT_ready")
        ge_ready = sem("ge_ready")
        off_ready = sem("off_ready")
        pos_ready = sem("pos_ready")
        sort_read = sem("sort_read")
        ea_arrived = [sem(f"ea_arrived{i}") for i in range(2)]
        staged = sem("staged")
        scattered = [sem(f"scattered{i}") for i in range(2)]
        s_staged = sem("s_staged")
        s_scattered = [sem(f"s_scattered{i}") for i in range(2)]
        last_staged = sem("last_staged")
        last_ea = sem("last_ea")
        last_scattered = sem("last_scattered")
        by_src_in = sem("by_src_in")
        hist_ready = sem("hist_ready")
        hist_used = sem("hist_used")
        hist_out = sem("hist_out")

        rec_arrived = [sem(f"rec_arrived{i}") for i in range(SLOTS)]
        rec_free = sem("rec_free")
        idx_ready = sem("idx_ready")
        gathered = [sem(f"gathered{i}") for i in range(SLOTS)]
        onehot_ready = sem("onehot_ready")
        rows_free = sem("rows_free")
        part_free = sem("part_free")
        ea_packed = sem("ea_packed")
        eaT_ps = sem("eaT_ps")
        eaT_sb = sem("eaT_sb")
        eaw_ready = sem("eaw_ready")
        pre_ready = sem("pre_ready")
        msg_ready = sem("msg_ready")
        pool_begun = sem("pool_begun")
        sums_begun = sem("sums_begun")
        table_ready = sem("table_ready")
        table_out = sem("table_out")
        std_in = sem("std_in")
        std_out = sem("std_out")
        hT_in = [sem(f"hT_in{i}") for i in range(5)]
        hT_ps = [sem(f"hT_ps{i}") for i in range(5)]
        hT_sb = [sem(f"hT_sb{i}") for i in range(5)]
        mlp_ps = sem("mlp_ps")
        mlp_hid = sem("mlp_hid")
        mlp_ps2 = sem("mlp_ps2")
        mlp_out = sem("mlp_out")
        bn_in = sem("bn_in")
        bn_std = sem("bn_std")
        bn_ready = sem("bn_ready")
        bn_out = sem("bn_out")
        back_ps = sem("back_ps")
        back_used = sem("back_used")
        proj_ps = [sem(f"proj_ps{i}") for i in range(4)]
        proj_used = [sem(f"proj_used{i}") for i in range(4)]
        rel_ps = [sem(f"rel_ps{i}") for i in range(2)]
        rel_a = [sem(f"rel_a{i}") for i in range(2)]
        rel_b = [sem(f"rel_b{i}") for i in range(2)]
        rel_out = [[sem(f"rel_out{i}_{j}") for j in range(2)] for i in range(2)]
        t_ps = sem("t_ps")
        root_in = sem("root_in")
        root_out = sem("root_out")
        t_pre = sem("t_pre")
        t_act = sem("t_act")
        silu_in = sem("silu_in")
        silu_out = sem("silu_out")
        y_ready = sem("y_ready")
        y_out = sem("y_out")

        def blocks(a, q=None, n=CB):
            v = a[:, :].rearrange("p (b f) -> p b f", f=D)
            return v if q is None else v[:, q * n:min(NB, (q + 1) * n), :]

        def by_node(s, lo=0, hi=NB):
            return s[:, lo:hi].unsqueeze(2).broadcast_to([P, hi - lo, D])

        def by_feature(r, n):
            return r.unsqueeze(1).broadcast_to([P, n, D])

        FIRST = {"L0": 0, "L1a": ROUNDS, "L1b": 2 * ROUNDS, "L2a": 3 * ROUNDS, "L2b": 4 * ROUNDS}
        L3_FIRST = 5 * ROUNDS

        block = ctx.enter_context(nc.Block())

        @block.sync
        def _(sp):
            for name, a in (("dst", dst), ("src", src), ("type", edge_type_8)):
                sp.dma_start(ints[name][:, 0:EC], a[0:EC * P].rearrange("(p c) -> p c", p=P)).then_inc(edges_in, 16)
                sp.dma_start(ints[name][0:ER, EC:ECP], a[EC * P:E].rearrange("(p c) -> p c", c=1)).then_inc(edges_in, 16)
            sp.wait_ge(memset_done, 1)
            sp.dma_start(blocks(xs)[:, 0:NB - 1, :], x[0:(NB - 1) * P, :].rearrange("(b p) f -> p b f", p=P)).then_inc(x_in, 16)
            sp.dma_start(blocks(xs)[0:LAST, NB - 1, :], x[(NB - 1) * P:N, :]).then_inc(x_in, 16)
            for k in range(8):
                n = RW * T // 8
                sp.dma_start(rec_dst_rows[:, k * n:(k + 1) * n], acc[:, 0:n].bitcast(I32)).then_inc(rec_zero, 16)
            sp.dma_start(rec_src_rows, acc[:, 0:SW * T].bitcast(I32)).then_inc(rec_zero, 16)
            for j in range(4):
                sp.dma_start(we_diag[j * ED:(j + 1) * ED, j * D:(j + 1) * D], L0_gnn_We).then_inc(weights_in, 16)
            for l in range(2):
                for b in range(BASES):
                    to = rw[l][b * SUB:(b + 1) * SUB, :].rearrange("i (r c) -> i r c", r=RELS)[:, :, b * SUB:(b + 1) * SUB]
                    sp.dma_start(to, L2_gnn_weights[l, :, b, :, :].rearrange("r i o -> i r o")).then_inc(weights_in, 16)
                sp.dma_start(lw[l][:, :], L2_gnn_loop_w[l, :, :]).then_inc(weights_in, 16)
                sp.dma_start(bias2[:, l, :], L2_gnn_bias[l:l + 1, :].broadcast_to([P, D])).then_inc(weights_in, 16)
            for to, a in ((w1a, L0_gnn_W1), (w2a, L0_gnn_W2), (w1b, L1_gnn_W1), (w2b, L1_gnn_W2)):
                sp.dma_start(to[:, :], a).then_inc(weights_in, 16)
            for j, a in enumerate((L0_gnn_b1, L0_gnn_b2, L0_gnn_gamma, L0_gnn_beta)):
                sp.dma_start(cols[:, j:j + 1], a.rearrange("(p c) -> p c", c=1)).then_inc(weights_in, 16)
            for to, a in ((be_row, L0_gnn_be), (b1_row, L1_gnn_b1), (b2_row, L1_gnn_b2), (be1_row, L1_gnn_be)):
                sp.dma_start(to[:, :], a.rearrange("(a f) -> a f", a=1).broadcast_to([P, D])).then_inc(weights_in, 16)
            sp.dma_start(we1[:, :, :], L1_gnn_We.rearrange("(c p) f -> p c f", p=P)).then_inc(weights_in, 16)
            sp.dma_start(t_col[:, :], L1_gnn_t_emb.rearrange("a (c p) -> p (a c)", p=P)).then_inc(weights_in, 16)

            ea_cols = edge_attr_32[0:EC * P, :].rearrange("(p c) f -> p (c f)", p=P)

            def load_ea(slot, at, used):
                if used is not None:
                    sp.wait_ge(staged, used)
                sp.dma_start(ea_in[:, slot, :], ea_cols[:, bass.ds(at, CH * ED)]).then_inc(ea_arrived[slot], 16)
            load_ea(0, 0, None)
            load_ea(1, CH * ED, None)
            with sp.Fori(0, (NCH - 3) // 2) as i:
                for slot in range(2):
                    load_ea(slot, (2 * i + 2 + slot) * (CH * ED), 2 * i + slot + 1)
            load_ea(0, (NCH - 1) * CH * ED, NCH - 2)
            sp.wait_ge(staged, NCH - 1)
            sp.dma_start(ea_in[0:ER, 1, 0:ED], edge_attr_32[EC * P:E, :]).then_inc(last_ea, 16)

            sp.wait_ge(table_ready, 1)
            sp.dma_start(table_rows, tab[:, :]).then_inc(table_out, 16)

            for i in range(2):
                sp.wait_ge(scattered[i], 16 * CH * ((NCH + 1 - i) // 2))
            sp.wait_ge(last_scattered, 16)
            with sp.Fori(0, ROUNDS) as it:
                for g in range(SLOTS):
                    sp.wait_ge(rec_free, it * SLOTS + g + 1)
                    sp.dma_start(rec_in[:, g, :, :].rearrange("p t w -> p (t w)"),
                                 rec_dst_rows[:, bass.ds((it * SLOTS + g) * (GT * RW), GT * RW)]).then_inc(rec_arrived[g], 16)

            for k in range(2):
                sp.wait_ge(table_ready, 2 + k)
                sp.dma_start(table_rows, tab[:, :]).then_inc(table_out, 16)
            for l in range(2):
                for b in range(NB):
                    sp.wait_ge(rel_a[l], b + 1)
                    sp.wait_ge(rel_b[l], b + 1)
                    sp.dma_start(table_rel_rows[:, b, :], rel_st[:, b % 2, :]).then_inc(rel_out[l][b % 2], 16)
            for i in range(2):
                sp.wait_ge(s_scattered[i], 16 * CH * ((NCH + 1 - i) // 2))
            sp.wait_ge(last_scattered, 32)
            sp.wait_ge(table_ready, 4)
            sp.dma_start(tile_rows[:, :], rec_src_rows).then_inc(by_src_in, 16)
            with sp.Fori(0, STEPS) as k:
                sp.wait_ge(table_ready, k + 4)
                sp.dma_start(table_rows, tab[:, :]).then_inc(table_out, 16)
            sp.wait_ge(y_ready, 1)
            sp.dma_start(out[0:(NB - 1) * P, :].rearrange("(b p) f -> p b f", p=P), blocks(xs)[:, 0:NB - 1, :]).then_inc(y_out, 16)
            sp.dma_start(out[(NB - 1) * P:N, :], blocks(xs)[0:LAST, NB - 1, :]).then_inc(y_out, 16)
            sp.wait_ge(y_out, 32)

        @block.gpsimd
        def _(pool):
            made = 0

            def const(ins):
                nonlocal made
                made += 1
                ins.then_inc(consts, 1)

            const(nc.gpsimd.memset(ident[:, :], 0.0))
            const(nc.gpsimd.memset(ones[:, :], 1.0))
            pool.wait_ge(consts, made)
            const(nc.gpsimd.affine_select(out=ident[:, :], in_=ident[:, :], compare_op=ALU.not_equal, fill=1.0,
                                          base=0, pattern=[[-1, P]], channel_multiplier=1))
            const(nc.gpsimd.affine_select(out=before[:, :], in_=ones[:, :], compare_op=ALU.is_gt, fill=0.0,
                                          base=0, pattern=[[1, P]], channel_multiplier=-1))
            const(nc.gpsimd.affine_select(out=upto[:, :], in_=ones[0:NB, 0:NB], compare_op=ALU.is_ge, fill=0.0,
                                          base=0, pattern=[[1, NB]], channel_multiplier=-1))
            const(nc.gpsimd.iota(places[:, :], pattern=[[0, GT], [1, P]], base=1, channel_multiplier=0,
                                 allow_small_or_imprecise_dtypes=True))
            const(nc.gpsimd.iota(blk_no[:, :], pattern=[[0, HC], [1, NB]], base=0, channel_multiplier=0,
                                 allow_small_or_imprecise_dtypes=True))
            const(nc.gpsimd.iota(tile_no[:, :], pattern=[[1, T]], base=0, channel_multiplier=0,
                                 allow_small_or_imprecise_dtypes=True))
            assert made == CONSTS

            def begin():
                pool.sem_inc(pool_begun, 1)

            at = bass.IndirectOffsetOnAxis

            def scatter_dst(slot, number):
                pool.wait_ge(staged, number)
                begin()
                for c in range(CH):
                    pool.indirect_dma_start(out=rec_dst, out_offset=at(ap=stage_pos[:, slot, c:c + 1], axis=0),
                                            in_=stage[:, slot, c, :], in_offset=None).then_inc(scattered[slot], 16)

            pool.wait_ge(rec_zero, 16 * 9)
            with pool.Fori(0, (NCH - 1) // 2) as i:
                for slot in range(2):
                    scatter_dst(slot, 2 * i + slot + 1)
            scatter_dst(0, NCH)
            pool.wait_ge(last_staged, 1)
            pool.indirect_dma_start(out=rec_dst, out_offset=at(ap=pos_dst[0:ER, EC:ECP], axis=0),
                                    in_=stage[0:ER, 1, 0, :], in_offset=None).then_inc(last_scattered, 16)

            def gather(g, source, index, width=D):
                for j in range(GT):
                    pool.indirect_dma_start(out=rows[:, g, j * D:(j + 1) * D], out_offset=None, in_=source,
                                            in_offset=at(ap=index(g, j), axis=0)).then_inc(gathered[g], 16)

            pool.wait_ge(table_out, 16)
            with pool.Fori(0, ROUNDS) as it:
                for g in range(SLOTS):
                    pool.wait_ge(rec_arrived[g], 16 * (it + 1))
                    pool.wait_ge(rows_free, it * SLOTS + g + 1)
                    begin()
                    gather(g, table, lambda g, j: rec_in[:, g, j, 0:1])

            def scatter_src(slot, number):
                pool.wait_ge(s_staged, number)
                begin()
                for c in range(CH):
                    pool.indirect_dma_start(out=rec_src, out_offset=at(ap=stage_pos[:, slot, c:c + 1], axis=0),
                                            in_=stage[:, slot, c, 0:SW], in_offset=None).then_inc(s_scattered[slot], 16)
            with pool.Fori(0, (NCH - 1) // 2) as i:
                for slot in range(2):
                    scatter_src(slot, 2 * i + slot + 1)
            scatter_src(0, NCH)
            pool.wait_ge(last_staged, 2)
            pool.indirect_dma_start(out=rec_src, out_offset=at(ap=pos_src[0:ER, EC:ECP], axis=0),
                                    in_=stage[0:ER, 1, 0, 0:SW], in_offset=None).then_inc(last_scattered, 16)

            def gather_all(source, first):
                with pool.Fori(0, ROUNDS) as it:
                    for g in range(SLOTS):
                        pool.wait_ge(idx_ready, (first - ROUNDS + it) * SLOTS + g + 1)
                        begin()
                        gather(g, source, lambda g, j: idx_st[:, g, j:j + 1])
            for n, site in enumerate(("L1a", "L1b")):
                pool.wait_ge(table_out, 16 * (2 + n))
                gather_all(table, FIRST[site])
            for l, site in enumerate(("L2a", "L2b")):
                for j in range(2):
                    pool.wait_ge(rel_out[l][j], 16 * ((NB + 1 - j) // 2))
                gather_all(table_rel, FIRST[site])
            with pool.Fori(0, STEPS) as k:
                pool.wait_ge(table_out, 16 * (k + 4))
                begin()
                gather_all(table, L3_FIRST + k * ROUNDS)

        @block.scalar
        def _(act):
            def std(number):
                act.wait_ge(std_in, number)
                nc.scalar.sqrt(rstd[:, :], rstd[:, :]).then_inc(std_out, 1)
            std(1)

            def put_together(slot, at_col, rnd, waits):
                act.wait_ge(ea_arrived[slot], 16 * rnd)
                if waits is not None:
                    act.wait_ge(scattered[slot], waits)
                nc.scalar.copy(stage[:, slot, :, 0:1], srow[:, bass.ds(at_col, CH)].unsqueeze(2))
                nc.scalar.copy(stage[:, slot, :, 1:2], rrow[:, bass.ds(at_col, CH)].unsqueeze(2))
                nc.scalar.copy(stage[:, slot, :, 2:3].bitcast(F32), dloc[:, bass.ds(at_col, CH)].unsqueeze(2))
                nc.scalar.copy(stage_pos[:, slot, :], pos_dst[:, bass.ds(at_col, CH)])
                nc.scalar.copy(stage[:, slot, :, 4:RW].bitcast(F32),
                               ea_in[:, slot, :].rearrange("p (c f) -> p c f", f=ED)).then_inc(staged, 1)

            act.wait_ge(pos_ready, 1)
            act.wait_ge(memset_done, 1)
            put_together(0, 0, 1, None)
            put_together(1, CH, 1, None)
            with act.Fori(0, (NCH - 3) // 2) as i:
                for slot in range(2):
                    put_together(slot, (2 * i + 2 + slot) * CH, i + 2, (i + 1) * (16 * CH))
            put_together(0, (NCH - 1) * CH, (NCH + 1) // 2, 16 * CH * ((NCH - 1) // 2))
            act.wait_ge(last_ea, 16)
            act.wait_ge(scattered[1], 16 * CH * ((NCH - 1) // 2))
            nc.scalar.copy(stage[0:ER, 1, 0, 0:1], srow[0:ER, EC:ECP])
            nc.scalar.copy(stage[0:ER, 1, 0, 1:2], rrow[0:ER, EC:ECP])
            nc.scalar.copy(stage[0:ER, 1, 0, 2:3].bitcast(F32), dloc[0:ER, EC:ECP])
            nc.scalar.copy(stage[0:ER, 1, 0, 4:RW].bitcast(F32), ea_in[0:ER, 1, 0:ED]).then_inc(last_staged, 1)

            act.sem_inc(rec_free, SLOTS)
            act.sem_inc(eaT_sb, 1)
            with act.Fori(0, ROUNDS) as it:
                for g in range(SLOTS):
                    G = it * SLOTS + g
                    act.wait_ge(rec_arrived[g], 16 * (it + 1))
                    t0 = G * GT
                    nc.scalar.copy(ea_flat[:, :].rearrange("p (t f) -> p t f", t=GT),
                                   rec_in[:, g, :, 4:RW].bitcast(F32)).then_inc(ea_packed, 1)
                    nc.scalar.copy(row_src[:, bass.ds(t0, GT)], rec_in[:, g, :, 0])
                    nc.scalar.copy(row_rel[:, bass.ds(t0, GT)], rec_in[:, g, :, 1])
                    nc.scalar.copy(loc_dst[:, bass.ds(t0, GT)], rec_in[:, g, :, 2].bitcast(F32))
                    for half in range(2):
                        act.wait_ge(eaT_ps, 2 * G + half + 1)
                        nc.scalar.copy(eaT[:, :], tbank[0][:, 0:P]).then_inc(eaT_sb, 1)
                    act.wait_ge(pre_ready, G + 2)
                    nc.scalar.activation(rows[:, g, :], rows[:, g, :], ACT.Relu).then_inc(msg_ready, 1)

            def put_src(slot, at_col, waits):
                if waits is not None:
                    act.wait_ge(s_scattered[slot], waits)
                nc.scalar.copy(stage[:, slot, :, 0:1], drow[:, bass.ds(at_col, CH)].unsqueeze(2))
                nc.scalar.copy(stage[:, slot, :, 1:2].bitcast(F32), sloc[:, bass.ds(at_col, CH)].unsqueeze(2))
                nc.scalar.copy(stage_pos[:, slot, :], pos_src[:, bass.ds(at_col, CH)]).then_inc(s_staged, 1)
            act.wait_ge(pos_ready, 2)
            act.wait_ge(last_scattered, 16)
            act.wait_ge(scattered[0], 16 * CH * ((NCH + 1) // 2))
            put_src(0, 0, None)
            put_src(1, CH, None)
            with act.Fori(0, (NCH - 3) // 2) as i:
                for slot in range(2):
                    put_src(slot, (2 * i + 2 + slot) * CH, (i + 1) * (16 * CH))
            put_src(0, (NCH - 1) * CH, 16 * CH * ((NCH - 1) // 2))
            act.wait_ge(s_scattered[1], 16 * CH * ((NCH - 1) // 2))
            nc.scalar.copy(stage[0:ER, 1, 0, 0:1], drow[0:ER, EC:ECP])
            nc.scalar.copy(stage[0:ER, 1, 0, 1:2].bitcast(F32), sloc[0:ER, EC:ECP]).then_inc(last_staged, 1)

            def keep_transposed(n):
                for q in range(NT):
                    act.wait_ge(hT_ps[n], q + 1)
                    w = min(4, NB - 4 * q) * P
                    nc.scalar.copy(hT[:, q * BANK:q * BANK + w], tbank[q % 2][0:D, 0:w]).then_inc(hT_sb[n], 1)

            keep_transposed(0)
            for q in range(NT):
                w = min(4, NB - 4 * q) * P
                at_q = slice(q * BANK, q * BANK + w)
                act.wait_ge(mlp_ps, q + 1)
                nc.scalar.activation(hT[:, at_q], part[q % 2][0:D, 0:w], ACT.Relu, bias=cols[:, 0:1]).then_inc(mlp_hid, 1)
                act.wait_ge(mlp_ps2, q + 1)
                nc.scalar.activation(hT[:, at_q], part[2 + q % 2][0:D, 0:w], ACT.Identity, bias=cols[:, 1:2]).then_inc(mlp_out, 1)
            act.wait_ge(bn_in, 1)
            nc.scalar.sqrt(bcol[:, 0:1], bcol[:, 0:1]).then_inc(bn_std, 1)
            act.wait_ge(bn_ready, 1)
            for q in range(NT):
                w = min(4, NB - 4 * q) * P
                at_q = slice(q * BANK, q * BANK + w)
                nc.scalar.activation(hT[:, at_q], hT[:, at_q], ACT.Relu, bias=bcol[:, 2:3],
                                     scale=bcol[:, 1:2]).then_inc(bn_out, 1)

            act.wait_ge(t_pre, 1)
            nc.scalar.activation(t_sig[:, :], t_row[:, :], ACT.Sigmoid).then_inc(t_act, 1)
            act.wait_ge(root_in, 1)
            nc.scalar.sqrt(factors[:, :, :], factors[:, :, :]).then_inc(root_out, 1)
            std(2)

            def stage_rows(first, source):
                act.wait_ge(msg_ready, GROUPS)
                with act.Fori(0, ROUNDS) as it:
                    for g in range(SLOTS):
                        G = (first + it) * SLOTS + g
                        act.wait_ge(rows_free, G + 1)
                        nc.scalar.copy(idx_st[:, g, :], source(it * (SLOTS * GT) + g * GT)).then_inc(idx_ready, 1)

            keep_transposed(1)
            stage_rows(FIRST["L1a"], lambda t: row_src[:, bass.ds(t, GT)])
            keep_transposed(2)
            stage_rows(FIRST["L1b"], lambda t: row_src[:, bass.ds(t, GT)])
            act.wait_ge(silu_in, 1)
            nc.scalar.activation(acc[:, :], tab[:, :], ACT.Sigmoid).then_inc(silu_out, 1)
            std(3)
            for l, site in enumerate(("L2a", "L2b")):
                keep_transposed(3 + l)
                for b in range(NB):
                    act.wait_ge(rel_ps[l], b + 1)
                    if b >= 2:
                        act.wait_ge(rel_out[l][b % 2], 16 * (b // 2))
                    lo = (tbank if b % 2 else pbank)[0]
                    nc.scalar.copy(rel_st[:, b % 2, 0:4 * D], lo[:, 0:4 * D]).then_inc(rel_a[l], 1)
                stage_rows(FIRST[site], lambda t: row_rel[:, bass.ds(t, GT)])
            std(4)
            act.wait_ge(by_src_in, 16)
            with act.Fori(0, STEPS) as k:
                stage_rows(L3_FIRST + k * ROUNDS, lambda t: by_src[:, bass.ds(t, GT), 0])

        @block.tensor
        def _(pe):
            pe.sem_inc(rows_free, SLOTS)
            pe.wait_ge(consts, CONSTS)
            for k in range(2):
                pe.wait_ge(cnt_ready, k + 1)
                nc.tensor.matmul(pbank[0][:, 0:NB], ones[:, :], cnt[:, :], start=True, stop=True)
                nc.tensor.matmul(pbank[1][:, 0:NB], before[:, :], cnt[:, :], start=True, stop=True)
                nc.tensor.matmul(tbank[0][0:NB, 0:1], cnt[:, :], ones[:, 0:1], start=True, stop=True).then_inc(tot_ready, 1)
                pe.wait_ge(tilesT_ready, k + 1)
                nc.tensor.matmul(tbank[1][0:NB, 0:1], upto[:, :], totT[:, :], start=True, stop=True).then_inc(endT_ready, 1)
                pe.wait_ge(ge_ready, k + 1)
                for half in range(2):
                    last = nc.tensor.matmul(part[half][0:1, 0:T // 2], ones[0:NB, 0:1],
                                            tile_ge[:, half * (T // 2):(half + 1) * (T // 2)], start=True, stop=True)
                last.then_inc(off_ready, 1)
            for k in range(2):
                hist = pbank[k][:, 0:NB]

                def count(slot, number, columns, start=False, stop=False):
                    pe.wait_ge(hist_ready, number)
                    for c in range(columns):
                        last = nc.tensor.matmul(hist, oh_loc[:, slot, c, :], oh_blk[:, slot, c, :],
                                                start=start and c == 0, stop=stop)
                    last.then_inc(hist_used, 1)
                count(0, (HS + 1) * k + 1, HC, start=True)
                with pe.Fori(0, HS // 2) as i:
                    for s in range(2):
                        count(1 - s, (HS + 1) * k + 2 + 2 * i + s, HC)
                count(1, (HS + 1) * (k + 1), 1, stop=True)

            def scatter_add(g, G):
                pe.wait_ge(onehot_ready, G + 1)
                pe.wait_ge(part_free, G + 1)
                for j in range(GT):
                    to = part[2 * (g % 2) + j // 4][:, (j % 4) * D:(j % 4 + 1) * D]
                    last = nc.tensor.matmul(to, onehot[:, g % 2, j * P:(j + 1) * P],
                                            rows[:, g, j * D:(j + 1) * D], start=True, stop=True)
                last.then_inc(rows_free, 1)

            pe.wait_ge(weights_in, 16 * WEIGHTS)
            pe.wait_ge(hist_out, 1)
            with pe.Fori(0, ROUNDS) as it:
                for g in range(SLOTS):
                    G = it * SLOTS + g
                    pe.wait_ge(ea_packed, G + 1)
                    for half in range(2):
                        pe.wait_ge(eaT_sb, 2 * G + half + 1)
                        nc.tensor.transpose(tbank[0][:, 0:P], ea_flat[:, half * P:(half + 1) * P],
                                            ident[:, :]).then_inc(eaT_ps, 1)
                        pe.wait_ge(eaT_sb, 2 * G + half + 2)
                        pe.wait_ge(pre_ready, G + 1)
                        last = nc.tensor.matmul(pbank[half][:, 0:4 * D], eaT[:, :], we_diag[:, :], start=True, stop=True)
                    last.then_inc(eaw_ready, 1)
                    pe.wait_ge(msg_ready, G + 1)
                    scatter_add(g, G)

            def transpose_nodes(n, a):
                pe.wait_ge(hT_in[n], 1)
                for q in range(NT):
                    if q >= 2:
                        pe.wait_ge(hT_sb[n], q - 1)
                    for b in range(4 * q, min(NB, 4 * q + 4)):
                        last = nc.tensor.transpose(tbank[q % 2][0:D, (b - 4 * q) * P:(b - 4 * q + 1) * P],
                                                   a[:, b * D:(b + 1) * D], ident[:, :])
                    last.then_inc(hT_ps[n], 1)

            transpose_nodes(0, h)
            for q in range(NT):
                w = min(4, NB - 4 * q) * P
                at_q = slice(q * BANK, q * BANK + w)
                pe.wait_ge(hT_sb[0], NT)
                if q >= 2:
                    pe.wait_ge(mlp_out, q - 1)
                nc.tensor.matmul(part[q % 2][0:D, 0:w], w1a[:, :], hT[:, at_q], start=True, stop=True).then_inc(mlp_ps, 1)
                pe.wait_ge(mlp_hid, q + 1)
                nc.tensor.matmul(part[2 + q % 2][0:D, 0:w], w2a[:, :], hT[:, at_q], start=True, stop=True).then_inc(mlp_ps2, 1)
            for q in range(NQ):
                pe.wait_ge(bn_out, min(NT, -(-((q + 1) * CB) // 4)))
                if q >= 2:
                    pe.wait_ge(back_used, q - 1)
                for b in range(CB * q, min(NB, CB * q + CB)):
                    last = nc.tensor.transpose(pbank[q % 2][:, (b - CB * q) * D:(b - CB * q + 1) * D],
                                               hT[:, b * P:(b + 1) * P], ident[0:D, 0:D])
                last.then_inc(back_ps, 1)

            pe.wait_ge(back_used, NQ)
            for c in range(3):
                last = nc.tensor.matmul(pbank[0][:, 0:D], t_rep[:, c, :], we1[:, c, :], start=(c == 0), stop=(c == 2))
            last.then_inc(t_ps, 1)

            def project(n, w_, tn):
                for q in range(NQ):
                    pe.wait_ge(hT_sb[tn], NT)
                    if q >= 2:
                        pe.wait_ge(proj_used[n], q - 1)
                    for b in range(CB * q, min(NB, CB * q + CB)):
                        last = nc.tensor.matmul(pbank[q % 2][:, (b - CB * q) * D:(b - CB * q + 1) * D],
                                                hT[:, b * P:(b + 1) * P], w_[:, :], start=True, stop=True)
                    last.then_inc(proj_ps[n], 1)

            def sum_edges(first):
                with pe.Fori(0, ROUNDS) as it:
                    for g in range(SLOTS):
                        pe.wait_ge(gathered[g], (first + it + 1) * (16 * GT))
                        scatter_add(g, (first + it) * SLOTS + g)

            transpose_nodes(1, h)
            pe.wait_ge(t_pre, 1)
            project(0, w1b, 1)
            sum_edges(FIRST["L1a"])
            transpose_nodes(2, acc)
            project(1, w2b, 2)
            sum_edges(FIRST["L1b"])
            for l, site in enumerate(("L2a", "L2b")):
                transpose_nodes(3 + l, h)
                project(2 + l, lw[l], 3 + l)
                pe.wait_ge(proj_used[2 + l], NQ)
                for b in range(NB):
                    if b >= 2:
                        pe.wait_ge(rel_a[l], b - 1)
                        pe.wait_ge(rel_b[l], b - 1)
                    pair = tbank if b % 2 else pbank
                    for half in range(2):
                        last = nc.tensor.matmul(pair[half][:, 0:4 * D], hT[:, b * P:(b + 1) * P],
                                                rw[l][:, half * 4 * D:(half + 1) * 4 * D], start=True, stop=True)
                    last.then_inc(rel_ps[l], 1)
                sum_edges(FIRST[site])
            with pe.Fori(0, STEPS) as k:
                sum_edges(L3_FIRST + k * ROUNDS)

        @block.vector
        def _(dve):
            chain = Count(dve_step)

            def then(ins):
                chain.step(ins)
                dve.wait_ge(dve_step, chain.value)

            V = nc.vector
            V.memset(xs[:, (NB - 1) * D:W], 0.0)
            V.memset(we_diag[:, :], 0.0)
            V.memset(rw[0][:, :], 0.0)
            V.memset(rw[1][:, :], 0.0)
            V.memset(stage[:, :, :, :].bitcast(F32).rearrange("p s c w -> p (s c w)"), 0.0)
            V.memset(acc[:, :], 0.0).then_inc(memset_done, 1)
            dve.sem_inc(part_free, 2)
            dve.sem_inc(pre_ready, 1)

            def norm(number, relu_to):
                for b in range(NB):
                    V.bn_stats(stats[:, b, :], xs[:, b * D:(b + 1) * D]).then_inc(dve_step, 1)
                chain.value = chain.value + NB
                dve.wait_ge(dve_step, chain.value)
                for b in range(NB):
                    V.bn_aggr(mv[:, b, :], stats[:, b, :]).then_inc(dve_step, 1)
                chain.value = chain.value + NB
                dve.wait_ge(dve_step, chain.value)
                V.tensor_scalar(rstd[:, :], mv[:, :, 1], 1e-5, None, ALU.add).then_inc(std_in, 1)
                then(V.tensor_tensor(blocks(relu_to), blocks(xs), by_node(mv[:, :, 0]), ALU.subtract))
                dve.wait_ge(std_out, number)
                then(V.reciprocal(rstd[:, :], rstd[:, :]))
                then(V.tensor_tensor(blocks(relu_to), blocks(relu_to), by_node(rstd), ALU.mult))
                then(V.tensor_scalar(relu_to[:, :], relu_to[:, :], 0.0, None, ALU.max))

            dve.wait_ge(x_in, 32)
            norm(1, h)
            dve.wait_ge(weights_in, 16 * WEIGHTS)
            for c in range(3):
                then(V.tensor_copy(t_rep[:, c, :], t_col[:, c:c + 1].broadcast_to([P, P])))

            dve.wait_ge(edges_in, 16 * 6)
            dve.wait_ge(memset_done, 1)
            for key, loc, row in (("src", sloc, srow), ("dst", dloc, drow)):
                then(V.memset(blk[key][:, EC:ECP], 2.0 * NB))
                then(V.memset(loc[:, EC:ECP], 0.0))
                for lo, hi, n in ((0, EC, P), (EC, ECP, ER)):
                    a = ints[key][0:n, lo:hi]
                    then(V.tensor_scalar(low[0:n, lo:hi], a, P - 1, None, ALU.bitwise_and))
                    then(V.tensor_scalar(high[0:n, lo:hi], a, 7, None, ALU.logical_shift_right))
                    then(V.tensor_copy(blk[key][0:n, lo:hi], high[0:n, lo:hi]))
                    then(V.tensor_scalar(loc[0:n, lo:hi], low[0:n, lo:hi], 1.0, None, ALU.add))
                    then(V.scalar_tensor_tensor(row[0:n, lo:hi], low[0:n, lo:hi], float(NB), high[0:n, lo:hi],
                                                ALU.mult, ALU.add))
            for lo, hi, n in ((0, EC, P), (EC, ECP, ER)):
                then(V.scalar_tensor_tensor(rrow[0:n, lo:hi], srow[0:n, lo:hi], float(RELS),
                                            ints["type"][0:n, lo:hi], ALU.mult, ALU.add))

            dve.wait_ge(consts, CONSTS)

            def sort(k, key, pos, off):
                for b in range(NB):
                    then(V.tensor_scalar(cum, blk[key], float(b), 0.0, ALU.is_equal, ALU.add,
                                         accum_out=cnt[:, b:b + 1]))
                dve.sem_inc(cnt_ready, 1)
                dve.wait_ge(tot_ready, k + 1)
                then(V.tensor_scalar(totT_i[:, :], tbank[0][0:NB, 0:1], float(P - 1), None, ALU.add))
                then(V.tensor_scalar(totT_i[:, :], totT_i[:, :], 7, None, ALU.logical_shift_right))
                then(V.tensor_copy(totT[:, :], totT_i[:, :]))
                dve.sem_inc(tilesT_ready, 1)
                then(V.tensor_scalar(tot_i[:, :], pbank[0][:, 0:NB], float(P - 1), None, ALU.add))
                then(V.tensor_scalar(tot_i[:, :], tot_i[:, :], 7, None, ALU.logical_shift_right))
                then(V.tensor_copy(tot[:, :], tot_i[:, :]))
                then(V.tensor_tensor_scan(ends[:, :], tot[:, :], acc[:, 0:NB], 0.0, ALU.add, ALU.add))
                then(V.tensor_tensor(start[:, :], ends[:, :], tot[:, :], ALU.subtract))
                then(V.scalar_tensor_tensor(start[:, :], start[:, :], float(P), pbank[1][:, 0:NB], ALU.mult, ALU.add))
                then(V.tensor_scalar(start[:, :], start[:, :], -1.0, None, ALU.add))
                dve.wait_ge(endT_ready, k + 1)
                then(V.tensor_copy(endT[:, :], tbank[1][0:NB, 0:1]))
                then(V.tensor_scalar(tile_ge[:, :], tile_no[:, :], endT[:, 0:1], None, ALU.is_ge))
                dve.sem_inc(ge_ready, 1)
                dve.wait_ge(off_ready, k + 1)
                for half in range(2):
                    then(V.tensor_scalar(off[0:1, half * (T // 2):(half + 1) * (T // 2)], part[half][0:1, 0:T // 2],
                                         float(NB - 1), float(D), ALU.min, ALU.mult))
                for b in range(NB):
                    then(V.tensor_scalar(eq, blk[key], float(b), None, ALU.is_equal))
                    then(V.tensor_tensor_scan(cum, eq, zero_row, start[:, b:b + 1], ALU.add, ALU.add))
                    then(V.copy_predicated(pos_f, eq, cum))
                then(V.tensor_copy(low, pos_f))
                then(V.tensor_scalar(high, low, 7, None, ALU.logical_shift_right))
                then(V.tensor_scalar(low, low, P - 1, None, ALU.bitwise_and))
                V.scalar_tensor_tensor(pos[:, :], low, float(T), high, ALU.mult, ALU.add).then_inc(pos_ready, 1)
                dve.wait_ge(pos_ready, k + 1)

            then(V.memset(pos_f, 0.0))
            sort(0, "dst", pos_dst, off_dst)
            sort(1, "src", pos_src, off_src)

            def hist(k, key, loc):
                def make(slot, c0, n, used):
                    if used is not None:
                        dve.wait_ge(hist_used, used)
                    lc = places[:, 0:P].unsqueeze(1).broadcast_to([P, n, P])
                    bc = blk_no[:, 0:n * NB].rearrange("p (c b) -> p c b", c=n)
                    V.tensor_tensor(oh_loc[:, slot, 0:n, :], lc,
                                    loc[:, bass.ds(c0, n)].unsqueeze(2).broadcast_to([P, n, P]), ALU.is_equal)
                    V.tensor_tensor(oh_blk[:, slot, 0:n, :], bc,
                                    blk[key][:, bass.ds(c0, n)].unsqueeze(2).broadcast_to([P, n, NB]),
                                    ALU.is_equal).then_inc(hist_ready, 1)
                done = (HS + 1) * k
                make(0, 0, HC, done if k else None)
                make(1, HC, HC, None)
                make(0, 2 * HC, HC, done + 1)
                with dve.Fori(0, HS // 2 - 1) as i:
                    for s in range(2):
                        make(1 - s, (2 * i + s + 3) * HC, HC, done + 2 * i + s + 2)
                make(1, EC, 1, done + HS - 1)
            hist(0, "dst", dloc)
            hist(1, "src", sloc)
            dve.wait_ge(hist_used, 2 * (HS + 1))
            then(V.tensor_copy(deg["dst"][:, :], pbank[0][:, 0:NB]))
            then(V.tensor_copy(deg["src"][:, :], pbank[1][:, 0:NB]))
            dve.sem_inc(hist_out, 1)
            V.tensor_tensor(blocks(tab), blocks(h), by_feature(be_row[:, :], NB), ALU.add).then_inc(table_ready, 1)

            def make_onehot(g, G, places_of):
                dve.wait_ge(rows_free, G + SLOTS - 1)
                V.tensor_tensor(onehot[:, g % 2, :].rearrange("p (t n) -> p t n", t=GT),
                                places[:, :].rearrange("p (t n) -> p t n", t=GT),
                                places_of.unsqueeze(2).broadcast_to([P, GT, P]), ALU.is_equal).then_inc(onehot_ready, 1)

            def add_products(g, G, t0, off):
                _, to = nc.values_load_multi_w_load_instructions(
                    off[0:1, bass.ds(t0, GT)], engines=RAN, min_val=0, max_val=(NB - 1) * D,
                    skip_runtime_bounds_check_because="the offsets are clamped to the last block's when made")
                dve.wait_ge(rows_free, G + SLOTS + 1)
                for j in range(GT):
                    a = acc[:, bass.ds(to[j], D)]
                    p = part[2 * (g % 2) + j // 4][:, (j % 4) * D:(j % 4 + 1) * D]
                    then(V.tensor_tensor(a, a, p, ALU.add))
                dve.sem_inc(part_free, 1)

            with dve.Fori(0, ROUNDS) as it:
                chain.enter(it, SLOTS * GT)
                for g in range(SLOTS):
                    G = it * SLOTS + g
                    dve.wait_ge(rec_arrived[g], 16 * (it + 1))
                    make_onehot(g, G, rec_in[:, g, :, 2].bitcast(F32))
                    dve.wait_ge(gathered[g], (it + 1) * (16 * GT))
                    dve.wait_ge(eaw_ready, G + 1)
                    for half in range(2):
                        a = rows[:, g, half * 4 * D:(half + 1) * 4 * D]
                        last = V.tensor_tensor(a, a, pbank[half][:, 0:4 * D], ALU.add)
                    last.then_inc(pre_ready, 1)
                    add_products(g, G, it * (SLOTS * GT) + g * GT, off_dst)
                    dve.wait_ge(msg_ready, G + 1)
                    dve.sem_inc(rec_free, 1)
                chain.leave(ROUNDS)

            def sum_edges(first, off, places_of, nested=None):
                with dve.Fori(0, ROUNDS) as it:
                    chain.enter(it, SLOTS * GT)
                    for g in range(SLOTS):
                        G = (first + it) * SLOTS + g
                        t0 = it * (SLOTS * GT) + g * GT
                        make_onehot(g, G, places_of(t0))
                        add_products(g, G, t0, off)
                    chain.leave(ROUNDS)

            V.tensor_tensor(h[:, :], h[:, :], acc[:, :], ALU.add).then_inc(hT_in[0], 1)
            for q in range(NT):
                w = min(P * 4, N - q * BANK)
                dve.wait_ge(mlp_out, q + 1)
                V.bn_stats(bstats[:, q, :], hT[:, q * BANK:q * BANK + w]).then_inc(dve_step, 1)
            chain.value = chain.value + NT
            dve.wait_ge(dve_step, chain.value)
            then(V.bn_aggr(bmv[:, :], bstats[:, :, :].rearrange("p q s -> p (q s)")))
            V.tensor_scalar(bcol[:, 0:1], bmv[:, 1:2], 1e-5, None, ALU.add).then_inc(bn_in, 1)
            dve.wait_ge(bn_std, 1)
            then(V.reciprocal(bcol[:, 3:4], bcol[:, 0:1]))
            then(V.tensor_tensor(bcol[:, 1:2], bcol[:, 3:4], cols[:, 2:3], ALU.mult))
            then(V.tensor_tensor(bcol[:, 3:4], bmv[:, 0:1], bcol[:, 1:2], ALU.mult))
            V.tensor_tensor(bcol[:, 2:3], cols[:, 3:4], bcol[:, 3:4], ALU.subtract).then_inc(bn_ready, 1)
            for q in range(NQ):
                n = min(CB, NB - CB * q)
                dve.wait_ge(back_ps, q + 1)
                a = blocks(xs, q)
                V.tensor_tensor(a, a, pbank[q % 2][:, 0:n * D].rearrange("p (b f) -> p b f", f=D), ALU.add).then_inc(back_used, 1)
            dve.wait_ge(back_used, NQ)

            then(V.tensor_scalar(dinv, deg["dst"][:, :], 1.0, None, ALU.add))
            then(V.tensor_scalar(norm2[:, :], deg["dst"][:, :], 1.0, None, ALU.max))
            then(V.tensor_scalar(w_row, deg["src"][:, :], 1.0, None, ALU.max))
            then(V.tensor_copy(w_col, norm2[:, :]))
            then(V.reciprocal(norm2[:, :], norm2[:, :]))
            dve.wait_ge(t_ps, 1)
            then(V.tensor_tensor(t_row[:, :], pbank[0][:, 0:D], be1_row[:, :], ALU.add))
            dve.sem_inc(t_pre, 1)
            dve.wait_ge(t_act, 1)
            then(V.tensor_tensor(t_row[:, :], t_row[:, :], t_sig[:, :], ALU.mult))
            then(V.tensor_tensor(b1_row[:, :], b1_row[:, :], t_row[:, :], ALU.add))
            dve.sem_inc(root_in, 1)
            dve.wait_ge(root_out, 1)
            then(V.reciprocal(factors[:, :, :], factors[:, :, :]))
            norm(2, h)
            dve.sem_inc(hT_in[1], 1)

            def projected(n, scale, row):
                for q in range(NQ):
                    m = min(CB, NB - CB * q)
                    dve.wait_ge(proj_ps[n], q + 1)
                    p = pbank[q % 2][:, 0:m * D].rearrange("p (b f) -> p b f", f=D)
                    if scale is not None:
                        V.tensor_tensor(blocks(tab, q), p, by_node(scale, CB * q, CB * q + m), ALU.mult).then_inc(proj_used[n], 1)
                    else:
                        V.tensor_tensor(blocks(tab, q), p, by_feature(row, m), ALU.add).then_inc(proj_used[n], 1)
                dve.wait_ge(proj_used[n], NQ)

            for n, row in ((0, b1_row), (1, b2_row)):
                projected(n, dinv, None)
                dve.sem_inc(table_ready, 1)
                then(V.memset(acc[:, :], 0.0))
                sum_edges(FIRST["L1a" if n == 0 else "L1b"], off_dst, lambda t: loc_dst[:, bass.ds(t, GT)])
                to = tab if n else acc
                then(V.tensor_tensor(acc[:, :], acc[:, :], tab[:, :], ALU.add))
                then(V.tensor_tensor(blocks(acc), blocks(acc), by_node(dinv), ALU.mult))
                then(V.tensor_tensor(blocks(to), blocks(acc), by_feature(row[:, :], NB), ALU.add))
                dve.sem_inc(silu_in if n else hT_in[2], 1)
            dve.wait_ge(silu_out, 1)
            then(V.tensor_tensor(tab[:, :], tab[:, :], acc[:, :], ALU.mult))
            then(V.tensor_tensor(tab[:, :], tab[:, :], h[:, :], ALU.add))
            then(V.tensor_tensor(xs[:, :], xs[:, :], tab[:, :], ALU.add))
            norm(3, h)
            for l, site in enumerate(("L2a", "L2b")):
                dve.sem_inc(hT_in[3 + l], 1)
                projected(2 + l, None, bias2[:, l, :])
                for b in range(NB):
                    dve.wait_ge(rel_ps[l], b + 1)
                    if b >= 2:
                        dve.wait_ge(rel_out[l][b % 2], 16 * (b // 2))
                    hi = (tbank if b % 2 else pbank)[1]
                    V.tensor_copy(rel_st[:, b % 2, 4 * D:8 * D], hi[:, 0:4 * D]).then_inc(rel_b[l], 1)
                then(V.memset(acc[:, :], 0.0))
                sum_edges(FIRST[site], off_dst, lambda t: loc_dst[:, bass.ds(t, GT)])
                then(V.tensor_tensor(blocks(acc), blocks(acc), by_node(norm2), ALU.mult))
                then(V.tensor_tensor(acc[:, :], acc[:, :], tab[:, :], ALU.add))
                if l == 0:
                    then(V.tensor_scalar(h[:, :], acc[:, :], 0.0, None, ALU.max))
                else:
                    then(V.tensor_tensor(xs[:, :], xs[:, :], acc[:, :], ALU.add))
            norm(4, h)
            then(V.tensor_tensor(blocks(tab), blocks(h), by_node(w_col), ALU.mult))
            then(V.tensor_scalar(h[:, :], h[:, :], ALPHA, None, ALU.mult))
            then(V.tensor_scalar(w_row, w_row, BETA, None, ALU.mult))
            dve.sem_inc(table_ready, 1)
            dve.wait_ge(by_src_in, 16)
            with dve.Fori(0, STEPS) as k:
                chain.enter(k, T + 4)
                then(V.memset(acc[:, :], 0.0))
                dve.sem_inc(sums_begun, 1)
                sum_edges(L3_FIRST + k * ROUNDS, off_src, lambda t: by_src[:, bass.ds(t, GT), 1].bitcast(F32))
                then(V.tensor_tensor(blocks(acc), blocks(acc), by_node(w_row), ALU.mult))
                then(V.tensor_tensor(acc[:, :], acc[:, :], h[:, :], ALU.add))
                then(V.tensor_tensor(blocks(tab), blocks(acc), by_node(w_col), ALU.mult))
                dve.sem_inc(table_ready, 1)
                chain.leave(STEPS)
            then(V.tensor_scalar(acc[:, :], acc[:, :], 1.0 / THETA, None, ALU.mult))
            V.tensor_tensor(xs[:, :], xs[:, :], acc[:, :], ALU.add).then_inc(y_ready, 1)

_INS = ["x", "src", "dst", "edge_attr_32", "edge_type_8", "L0_gnn_We", "L0_gnn_be", "L0_gnn_W1", "L0_gnn_b1",
        "L0_gnn_W2", "L0_gnn_b2", "L0_gnn_gamma", "L0_gnn_beta", "L1_gnn_t_emb", "L1_gnn_W1", "L1_gnn_b1",
        "L1_gnn_W2", "L1_gnn_b2", "L1_gnn_We", "L1_gnn_be", "L2_gnn_weights", "L2_gnn_loop_w", "L2_gnn_bias"]

def kernel(**inputs):
    import numpy as _np
    import concourse.bacc as _bacc
    from concourse import mybir as _mybir
    from concourse.bass_utils import run_bass_kernel_spmd as _run

    nc = _bacc.Bacc("TRN2", target_bir_lowering=False, num_devices=1)
    arrays, args = {}, []
    for name in _INS:
        a = _np.ascontiguousarray(inputs[name])
        arrays[f"in_{name}"] = a
        args.append(nc.dram_tensor(f"in_{name}", a.shape, _mybir.dt.from_np(a.dtype), kind="ExternalInput").ap())
    args.append(nc.dram_tensor("out_x", (N, D), _mybir.dt.float32, kind="ExternalOutput").ap())
    build(nc, *args)
    r = _run(nc, [arrays], core_ids=[0])
    return r.results[0]["out_x"]
```

```python
import concourse.bass as bass
from concourse import mybir
from contextlib import ExitStack

F32, I32 = mybir.dt.float32, mybir.dt.int32
F16, F8, U8 = mybir.dt.float16, mybir.dt.float8e4, mybir.dt.uint8
ALU, ACT = mybir.AluOpType, mybir.ActivationFunctionType
X = mybir.AxisListType.X

P = 128
N, D, E = 6250, 96, 100000
NB = -(-N // P)
LAST = N - (NB - 1) * P
W = NB * D
ED = 32
RELS, BASES = 8, 8
SUB = D // BASES
T_DIM = 384
STEPS = 10
ALPHA, BETA = 0.1, 0.9
THETA = BETA ** STEPS + ALPHA * sum(BETA ** i for i in range(STEPS))

EC = E // P
ER = E - EC * P
ECP = EC + 1
CH = 71
NCH = EC // CH
assert NCH * CH == EC and NCH % 2 == 1

GT = 8
SLOTS = 4
T = 832
assert T >= E // P + NB and T % (GT * SLOTS) == 0
ROUNDS = T // (GT * SLOTS)
PADT = GT
GROUPS = T // GT
RW = 36
SW = 2
BANK = 512
CB = BANK // D
NQ = -(-NB // CB)
NT = -(-NB // 4)
HC = 11
HS = EC // HC
assert HS * HC == EC and HS % 2 == 1
CONSTS = 8
WEIGHTS = 4 + 2 * (BASES + 2) + 4 + 4 + 4 + 2
SB = 7
SG = NB // SB
assert SG * SB == NB and SG == 7
GC = SB * P
PG = 2
HALF = GC // 2
PC = PG * GC
RING = 4
MOST = 16
ZS = 64.0


class Count:

    def __init__(self, sem):
        self.sem, self.value, self.kept = sem, 0, []

    def step(self, instruction):
        instruction.then_inc(self.sem, 1)
        self.value = self.value + 1

    def enter(self, i, per):
        self.kept.append((self.value, per))
        self.value = self.value + i * per
        self.at = self.value

    def leave(self, trips):
        before, per = self.kept.pop()
        self.value = before + per * trips

def build(nc, x, src, dst, edge_attr_32, edge_type_8, L0_gnn_We, L0_gnn_be, L0_gnn_W1, L0_gnn_b1,
          L0_gnn_W2, L0_gnn_b2, L0_gnn_gamma, L0_gnn_beta, L1_gnn_t_emb, L1_gnn_W1, L1_gnn_b1,
          L1_gnn_W2, L1_gnn_b2, L1_gnn_We, L1_gnn_be, L2_gnn_weights, L2_gnn_loop_w, L2_gnn_bias, out):
    ctx = ExitStack()
    with ctx:
        ctx.enter_context(nc.allow_non_contiguous_dma("small weights, transposed on the way"))

        def sb(name, shape, dt=F32):
            return ctx.enter_context(nc.sbuf_tensor(name, shape, dt))

        def sem(name):
            return ctx.enter_context(nc.semaphore(name))

        rec_dst = nc.dram_tensor("rec_dst", (P * T, RW), I32).ap()
        rec_src = nc.dram_tensor("rec_src", (P * T, SW), I32).ap()
        table = nc.dram_tensor("node_table", (P * NB, D), F32).ap()
        table_rel = nc.dram_tensor("relation_table", (P * NB * RELS, D), F32).ap()
        table_rows = table.rearrange("(p b) f -> p (b f)", p=P)
        table_rel_rows = table_rel.rearrange("(p b r) f -> p b (r f)", p=P, b=NB)
        counts = nc.dram_tensor("edge_counts", (SG, P, NB * GC), U8).ap()
        rec_dst_rows = rec_dst.rearrange("(p t) w -> p (t w)", p=P)
        rec_src_rows = rec_src.rearrange("(p t) w -> p (t w)", p=P)

        xs = sb("x_residual", [P, W])
        h = sb("h", [P, W])
        acc = sb("edge_sums", [P, W])
        tab = sb("own_term", [P, W])
        hT_whole = sb("h_transposed", [P, NB * P])
        hT = hT_whole[0:D, :]

        tile_rows = sb("table_rows_of_tiles", [P, 2 * T], I32)
        row_src, row_rel = tile_rows[:, 0:T], tile_rows[:, T:2 * T]
        src_col = sb("source_column", [P, T])
        by_src = tile_rows[:, :].rearrange("p (t w) -> p t w", w=SW)
        loc_dst = sb("place_of_target", [P, T])
        tiles_dst = sb("block_of_tile_dst", [1, T + 2 * PADT], I32)
        tiles_src = sb("block_of_tile_src", [1, T + 2 * PADT], I32)
        pos_dst = sb("record_row_dst", [P, ECP], I32)
        pos_src = sb("record_row_src", [P, ECP], I32)
        srow, rrow, dloc = tile_rows[:, 0:ECP], tile_rows[:, ECP:2 * ECP], loc_dst[:, 0:ECP]
        drow = sb("edge_target_row", [P, ECP], I32)
        sloc = sb("edge_source_place", [P, ECP])

        def work(k, dt=F32):
            whole, k = (tab, k) if k < 6 else (hT_whole, k)
            lo = k * ECP if k < 6 else 2 * CH * ED + (k - 6) * ECP
            v = whole[:, lo:lo + ECP]
            return v.bitcast(dt) if dt != F32 else v
        assert 6 * ECP <= W and 2 * CH * ED + 2 * ECP <= NB * P
        ints = {"src": work(0, I32), "dst": work(1, I32), "type": work(2, I32)}
        blk = {"src": work(3), "dst": work(4)}
        cum, eq, pos_f = work(5), work(6, I32), work(7)
        zero_row = acc[:, 0:ECP]
        ea_in = hT_whole[:, 0:2 * CH * ED].rearrange("p (s w) -> p s w", s=2)

        rows = sb("rows", [P, SLOTS, GT * D])
        flat = rows[:, :, :].rearrange("p s w -> p (s w)")
        low, high = flat[:, 0:ECP].bitcast(I32), flat[:, ECP:2 * ECP].bitcast(I32)
        onehot = sb("onehot", [P, 2, GT * P])
        idx_st = sb("staged_rows", [P, SLOTS, GT], I32)
        rec_in = sb("records_in", [P, SLOTS, GT, RW], I32)
        stage = sb("staged_records", [P, 2, CH, RW], I32)
        stage_pos = sb("staged_record_rows", [P, 2, CH], I32)
        ea_flat = sb("edge_features_packed", [P, GT * ED])
        eaT = sb("edge_features_T", [P, P])
        rel_st = stage[:, 0, 0:2 * RELS * D // RW + 1, :].rearrange("p c w -> p (c w)")[:, 0:2 * RELS * D].bitcast(F32).rearrange("p (s w) -> p s w", s=2)

        def bytes_of(a, lo, n, dt):
            size = 2 if dt == F16 else 1 if dt == F8 else 4
            return a[:, lo // 4:(lo + n * size) // 4].bitcast(dt) if dt != F32 else a[:, lo // 4:lo // 4 + n]
        cols_oh = [bytes_of(hT_whole, i * PC * 2, PC, F16) for i in range(RING)]
        rows_oh = [bytes_of(hT_whole, RING * PC * 2 + i * P * 2, P, F16) for i in range(RING)]
        whole_counts = bytes_of(hT_whole, RING * (PC + P) * 2, PC, F16)
        over_out = bytes_of(hT_whole, RING * (PC + P) * 2 + PC * 2, PC, F16)
        counted = bytes_of(hT_whole, RING * (PC + P) * 2 + PC * 4, PC, F8)
        assert RING * (PC + P) * 2 + PC * 5 <= NB * P * 4
        stage_f = stage[:, :, :, :].rearrange("p s c w -> p (s c w)").bitcast(F32)
        rel_bytes = 2 * RELS * D * 4
        col_no = bytes_of(stage_f, rel_bytes, PC, F16)
        assert rel_bytes + PC * 2 <= 2 * CH * RW * 4
        over = sb("over_16", [P, NB * 4])
        slot_bytes = SB * GC
        slots = [bytes_of(hT_whole, i * slot_bytes, slot_bytes, F8) for i in range(4)] \
            + [bytes_of(stage_f, i * slot_bytes, slot_bytes, F8) for i in range(3)]
        z = tab[:, :].bitcast(F16).rearrange("p (b f) -> p b f", f=2 * D)
        sums = flat[:, 0:SB * 2 * D].rearrange("p (b f) -> p b f", f=2 * D)
        total = flat[:, SB * 2 * D:SB * 3 * D]

        ident = sb("ident", [P, P])
        ones = sb("ones", [P, P])
        before = sb("before", [P, P])
        upto = sb("upto", [NB, NB])
        places = sb("places", [P, GT * P])
        tile_no = flat[0:NB, 2 * ECP:2 * ECP + T]
        tile_ge = rec_in[0:NB, :, :, :].rearrange("p s t w -> p (s t w)")[:, 0:T].bitcast(F32)
        we_diag = sb("We_diag", [P, 4 * D])
        w1a = sb("L0_W1", [D, D])
        w2a = sb("L0_W2", [D, D])
        w1b = sb("L1_W1", [D, D])
        w2b = sb("L1_W2", [D, D])
        cols = sb("L0_columns", [D, 4])
        rw = [sb(f"relation_W{i}", [D, RELS * D]) for i in range(2)]
        lw = [sb(f"loop_W{i}", [D, D]) for i in range(2)]
        bias2 = sb("L2_bias", [P, 2, D])
        be_row = sb("be_row", [P, D])
        b1_row = sb("L1_b1_row", [P, D])
        b2_row = sb("L1_b2_row", [P, D])
        be1_row = sb("L1_be_row", [P, D])
        t_rep = sb("t_emb_rep", [P, 3, P])
        t_col = sb("t_emb_col", [P, 3])
        we1 = sb("L1_We", [P, 3, D])
        t_row = sb("t_row", [P, D])
        t_sig = sb("t_sig", [P, D])
        cnt = sb("cnt", [P, NB])
        tot = sb("tot", [P, NB])
        tot_i = sb("tot_i", [P, NB], I32)
        ends = sb("ends", [P, NB])
        start = sb("start", [P, NB])
        totT = sb("totT", [NB, 1])
        totT_i = sb("totT_i", [NB, 1], I32)
        endT = sb("endT", [NB, 1])
        deg = {"dst": sb("deg_dst", [P, NB]), "src": sb("deg_src", [P, NB])}
        factors = sb("node_factors", [P, 3, NB])
        dinv, w_row, w_col = factors[:, 0, :], factors[:, 1, :], factors[:, 2, :]
        norm2 = sb("node_norm", [P, NB])
        stats = sb("stats", [P, NB, 6])
        mv = sb("mean_var", [P, NB, 2])
        rstd = sb("rstd", [P, NB])
        bstats = sb("bstats", [D, NT, 6])
        bmv = sb("bmv", [D, 2])
        bcol = sb("bcol", [D, 4])
        hist_room = onehot[:, :, :].rearrange("p s w -> p (s w)").bitcast(mybir.dt.bfloat16)
        oh_loc = hist_room[:, 0:2 * HC * P].rearrange("p (s c n) -> p s c n", s=2, c=HC)
        oh_blk = hist_room[:, 2 * HC * P:2 * HC * (P + NB)].rearrange("p (s c b) -> p s c b", s=2, c=HC)
        blk_no = flat[:, 2 * ECP + T:2 * ECP + T + HC * NB]

        place_no = sb("place_no", [P, P], F16)
        minus = sb("minus_16", [P, 1])
        most = sb("most", [P, 1])
        flag = sb("flag", [1, 1], I32)
        f1 = sb("L3_factor", [P, NB])
        f2 = sb("L3_last_factor", [P, NB])
        banks = [ctx.enter_context(nc.psum_tensor(f"bank{i}", [P, BANK], F32)) for i in range(8)]
        wide = banks[0:4]
        tbank, pbank, part = banks[0:2], banks[2:4], banks[4:8]
        summed = banks[7][:, 0:D]

        consts = sem("consts")
        edges_in = sem("edges_in")
        x_in = sem("x_in")
        weights_in = sem("weights_in")
        memset_done = sem("memset_done")
        rec_zero = sem("rec_zero")
        dve_step = sem("dve_step")
        cnt_ready = sem("cnt_ready")
        tot_ready = sem("tot_ready")
        tilesT_ready = sem("tilesT_ready")
        endT_ready = sem("endT_ready")
        ge_ready = sem("ge_ready")
        off_ready = sem("off_ready")
        pos_ready = sem("pos_ready")
        sort_read = sem("sort_read")
        ea_arrived = [sem(f"ea_arrived{i}") for i in range(2)]
        staged = sem("staged")
        scattered = [sem(f"scattered{i}") for i in range(2)]
        s_staged = sem("s_staged")
        s_scattered = [sem(f"s_scattered{i}") for i in range(2)]
        last_staged = sem("last_staged")
        last_ea = sem("last_ea")
        last_scattered = sem("last_scattered")
        by_src_in = sem("by_src_in")
        hist_ready = sem("hist_ready")
        hist_used = sem("hist_used")
        hist_out = sem("hist_out")

        idx_in = [sem(f"idx_in{i}") for i in range(SLOTS)]
        col_no_made = sem("col_no_made")
        kept = sem("kept")
        packed = sem("packed")
        checked = sem("checked")
        tiles_known = sem("tiles_known")
        oh_ready = sem("count_onehot_ready")
        oh_free = sem("count_onehot_free")
        act_begun = sem("act_begun")
        dve_begun = sem("dve_begun")
        counts_out = [sem(f"counts_out{i}") for i in range(4)]
        most_ready = sem("most_ready")
        most_ps = sem("most_ps")
        flag_ready = sem("flag_ready")
        counts_in = [sem(f"counts_in{i}") for i in range(SG)]
        slot_free = sem("slot_free")
        bank_done = sem("bank_done")
        bank_free = sem("bank_free")
        sums_used = sem("sums_used")
        z_ready = sem("z_ready")
        pe_begun = sem("pe_begun")
        sp_begun = sem("sp_begun")
        general_step = sem("general_step")
        dense_step = sem("dense_step")

        rec_arrived = [sem(f"rec_arrived{i}") for i in range(SLOTS)]
        rec_free = sem("rec_free")
        gathered = [sem(f"gathered{i}") for i in range(SLOTS)]
        onehot_ready = sem("onehot_ready")
        rows_free = sem("rows_free")
        ea_packed = sem("ea_packed")
        eaT_ps = sem("eaT_ps")
        eaT_sb = sem("eaT_sb")
        eaw_ready = sem("eaw_ready")
        pre_ready = sem("pre_ready")
        msg_ready = sem("msg_ready")
        pool_begun = sem("pool_begun")
        table_ready = sem("table_ready")
        table_out = sem("table_out")
        std_in = sem("std_in")
        std_out = sem("std_out")
        hT_in = [sem(f"hT_in{i}") for i in range(5)]
        hT_ps = [sem(f"hT_ps{i}") for i in range(5)]
        hT_sb = [sem(f"hT_sb{i}") for i in range(5)]
        mlp_ps = sem("mlp_ps")
        mlp_hid = sem("mlp_hid")
        mlp_ps2 = sem("mlp_ps2")
        mlp_out = sem("mlp_out")
        bn_in = sem("bn_in")
        bn_std = sem("bn_std")
        bn_ready = sem("bn_ready")
        bn_out = sem("bn_out")
        back_ps = sem("back_ps")
        back_used = sem("back_used")
        proj_ps = [sem(f"proj_ps{i}") for i in range(4)]
        proj_used = [sem(f"proj_used{i}") for i in range(4)]
        rel_ps = [sem(f"rel_ps{i}") for i in range(2)]
        rel_a = [sem(f"rel_a{i}") for i in range(2)]
        rel_b = [sem(f"rel_b{i}") for i in range(2)]
        rel_out = [[sem(f"rel_out{i}_{j}") for j in range(2)] for i in range(2)]
        t_ps = sem("t_ps")
        root_in = sem("root_in")
        root_out = sem("root_out")
        t_pre = sem("t_pre")
        t_act = sem("t_act")
        silu_in = sem("silu_in")
        silu_out = sem("silu_out")
        y_ready = sem("y_ready")
        y_out = sem("y_out")

        def blocks(a, q=None, n=CB):
            v = a[:, :].rearrange("p (b f) -> p b f", f=D)
            return v if q is None else v[:, q * n:min(NB, (q + 1) * n), :]

        def by_node(s, lo=0, hi=NB):
            return s[:, lo:hi].unsqueeze(2).broadcast_to([P, hi - lo, D])

        def by_feature(r, n):
            return r.unsqueeze(1).broadcast_to([P, n, D])

        def blocks_of(eng, tiles, t0):
            def load(at, n, most):
                return nc.values_load_multi_w_load_instructions(
                    tiles[0:1, bass.ds(t0 + at, n)], engines=(eng.engine,), min_val=0, max_val=most,
                    skip_runtime_bounds_check_because="the blocks are clamped to the last one when they are made")[1]
            return load(PADT - 1, 1, NB) + load(PADT, GT, NB - 1), load(PADT + GT, 1, NB)

        FIRST = {"L0": 0, "L1a": ROUNDS, "L1b": 2 * ROUNDS, "L2a": 3 * ROUNDS, "L2b": 4 * ROUNDS}
        L3_FIRST = 5 * ROUNDS

        block = ctx.enter_context(nc.Block())

        @block.sync
        def _(sp):
            for name, a in (("dst", dst), ("src", src), ("type", edge_type_8)):
                sp.dma_start(ints[name][:, 0:EC], a[0:EC * P].rearrange("(p c) -> p c", p=P)).then_inc(edges_in, 16)
                sp.dma_start(ints[name][0:ER, EC:ECP], a[EC * P:E].rearrange("(p c) -> p c", c=1)).then_inc(edges_in, 16)
            sp.wait_ge(memset_done, 1)
            sp.dma_start(blocks(xs)[:, 0:NB - 1, :], x[0:(NB - 1) * P, :].rearrange("(b p) f -> p b f", p=P)).then_inc(x_in, 16)
            sp.dma_start(blocks(xs)[0:LAST, NB - 1, :], x[(NB - 1) * P:N, :]).then_inc(x_in, 16)
            for k in range(8):
                n = RW * T // 8
                sp.dma_start(rec_dst_rows[:, k * n:(k + 1) * n], acc[:, 0:n].bitcast(I32)).then_inc(rec_zero, 16)
            sp.dma_start(rec_src_rows, acc[:, 0:SW * T].bitcast(I32)).then_inc(rec_zero, 16)
            for j in range(4):
                sp.dma_start(we_diag[j * ED:(j + 1) * ED, j * D:(j + 1) * D], L0_gnn_We).then_inc(weights_in, 16)
            for l in range(2):
                for b in range(BASES):
                    to = rw[l][b * SUB:(b + 1) * SUB, :].rearrange("i (r c) -> i r c", r=RELS)[:, :, b * SUB:(b + 1) * SUB]
                    sp.dma_start(to, L2_gnn_weights[l, :, b, :, :].rearrange("r i o -> i r o")).then_inc(weights_in, 16)
                sp.dma_start(lw[l][:, :], L2_gnn_loop_w[l, :, :]).then_inc(weights_in, 16)
                sp.dma_start(bias2[:, l, :], L2_gnn_bias[l:l + 1, :].broadcast_to([P, D])).then_inc(weights_in, 16)
            for to, a in ((w1a, L0_gnn_W1), (w2a, L0_gnn_W2), (w1b, L1_gnn_W1), (w2b, L1_gnn_W2)):
                sp.dma_start(to[:, :], a).then_inc(weights_in, 16)
            for j, a in enumerate((L0_gnn_b1, L0_gnn_b2, L0_gnn_gamma, L0_gnn_beta)):
                sp.dma_start(cols[:, j:j + 1], a.rearrange("(p c) -> p c", c=1)).then_inc(weights_in, 16)
            for to, a in ((be_row, L0_gnn_be), (b1_row, L1_gnn_b1), (b2_row, L1_gnn_b2), (be1_row, L1_gnn_be)):
                sp.dma_start(to[:, :], a.rearrange("(a f) -> a f", a=1).broadcast_to([P, D])).then_inc(weights_in, 16)
            sp.dma_start(we1[:, :, :], L1_gnn_We.rearrange("(c p) f -> p c f", p=P)).then_inc(weights_in, 16)
            sp.dma_start(t_col[:, :], L1_gnn_t_emb.rearrange("a (c p) -> p (a c)", p=P)).then_inc(weights_in, 16)

            ea_cols = edge_attr_32[0:EC * P, :].rearrange("(p c) f -> p (c f)", p=P)

            def load_ea(slot, at, used):
                if used is not None:
                    sp.wait_ge(staged, used)
                sp.dma_start(ea_in[:, slot, :], ea_cols[:, bass.ds(at, CH * ED)]).then_inc(ea_arrived[slot], 16)
            load_ea(0, 0, None)
            load_ea(1, CH * ED, None)
            with sp.Fori(0, (NCH - 3) // 2) as i:
                for slot in range(2):
                    load_ea(slot, (2 * i + 2 + slot) * (CH * ED), 2 * i + slot + 1)
            load_ea(0, (NCH - 1) * CH * ED, NCH - 2)
            sp.wait_ge(staged, NCH - 1)
            sp.dma_start(ea_in[0:ER, 1, 0:ED], edge_attr_32[EC * P:E, :]).then_inc(last_ea, 16)

            sp.wait_ge(table_ready, 1)
            sp.dma_start(table_rows, tab[:, :]).then_inc(table_out, 16)

            for i in range(2):
                sp.wait_ge(scattered[i], 16 * CH * ((NCH + 1 - i) // 2))
            sp.wait_ge(last_scattered, 16)
            with sp.Fori(0, ROUNDS) as it:
                for g in range(SLOTS):
                    sp.wait_ge(rec_free, it * SLOTS + g + 1)
                    sp.dma_start(rec_in[:, g, :, :].rearrange("p t w -> p (t w)"),
                                 rec_dst_rows[:, bass.ds((it * SLOTS + g) * (GT * RW), GT * RW)]).then_inc(rec_arrived[g], 16)

            def stage_rows(first, source):
                with sp.Fori(0, ROUNDS) as it:
                    for g in range(SLOTS):
                        sp.wait_ge(rows_free, ((first + it) * SLOTS + g + 1) * GT)
                        sp.dma_start(idx_st[:, g, :], source(it * (SLOTS * GT) + g * GT)).then_inc(idx_in[g], 16)

            sp.wait_ge(msg_ready, GROUPS)
            for k, site in enumerate(("L1a", "L1b")):
                sp.wait_ge(table_ready, 2 + k)
                sp.dma_start(table_rows, tab[:, :]).then_inc(table_out, 16)
                stage_rows(FIRST[site], lambda t: row_src[:, bass.ds(t, GT)])
            for l, site in enumerate(("L2a", "L2b")):
                for b in range(NB):
                    sp.wait_ge(rel_a[l], b + 1)
                    sp.wait_ge(rel_b[l], b + 1)
                    sp.dma_start(table_rel_rows[:, b, :], rel_st[:, b % 2, :]).then_inc(rel_out[l][b % 2], 16)
                stage_rows(FIRST[site], lambda t: row_rel[:, bass.ds(t, GT)])

            sp.wait_ge(flag_ready, 1)
            over_most = sp.value_load(flag[0:1, 0:1], min_val=0, max_val=1)
            with sp.If(over_most == 0):
                for f in range(4):
                    sp.wait_ge(counts_out[f], 16 * (T + 1))
                with sp.Fori(0, STEPS) as k:
                    with sp.Fori(0, SG) as g:
                        n = k * SG + g
                        for c in range(SG):
                            if c < SG - 1:
                                sp.wait_ge(slot_free, n * (SG - 1) + c + 1)
                            else:
                                sp.wait_ge(bank_done, n * SB + SB)
                            sp.sem_inc(sp_begun, 1)
                            sp.dma_start(slots[c].bitcast(U8), counts[bass.ds(g, 1), :, c * slot_bytes:(c + 1) * slot_bytes]
                                         .rearrange("g p n -> (g p) n")).then_inc(counts_in[c], 16)
            with sp.Else():
                for i in range(2):
                    sp.wait_ge(s_scattered[i], 16 * CH * ((NCH + 1 - i) // 2))
                sp.wait_ge(last_scattered, 32)
                sp.dma_start(tile_rows[:, :], rec_src_rows).then_inc(by_src_in, 16)
                sp.wait_ge(by_src_in, 16)
                with sp.Fori(0, STEPS) as k:
                    sp.wait_ge(table_ready, k + 4)
                    sp.dma_start(table_rows, tab[:, :]).then_inc(table_out, 16)
                    stage_rows(L3_FIRST + k * ROUNDS, lambda t: by_src[:, bass.ds(t, GT), 0])
            sp.wait_ge(y_ready, 1)
            sp.dma_start(out[0:(NB - 1) * P, :].rearrange("(b p) f -> p b f", p=P), blocks(xs)[:, 0:NB - 1, :]).then_inc(y_out, 16)
            sp.dma_start(out[(NB - 1) * P:N, :], blocks(xs)[0:LAST, NB - 1, :]).then_inc(y_out, 16)
            sp.wait_ge(y_out, 32)

        @block.gpsimd
        def _(pool):
            made = 0

            def const(ins):
                nonlocal made
                made += 1
                ins.then_inc(consts, 1)

            const(nc.gpsimd.memset(ident[:, :], 0.0))
            const(nc.gpsimd.memset(ones[:, :], 1.0))
            pool.wait_ge(consts, made)
            const(nc.gpsimd.affine_select(out=ident[:, :], in_=ident[:, :], compare_op=ALU.not_equal, fill=1.0,
                                          base=0, pattern=[[-1, P]], channel_multiplier=1))
            const(nc.gpsimd.affine_select(out=before[:, :], in_=ones[:, :], compare_op=ALU.is_gt, fill=0.0,
                                          base=0, pattern=[[1, P]], channel_multiplier=-1))
            const(nc.gpsimd.affine_select(out=upto[:, :], in_=ones[0:NB, 0:NB], compare_op=ALU.is_ge, fill=0.0,
                                          base=0, pattern=[[1, NB]], channel_multiplier=-1))
            const(nc.gpsimd.iota(places[:, :], pattern=[[0, GT], [1, P]], base=1, channel_multiplier=0,
                                 allow_small_or_imprecise_dtypes=True))
            const(nc.gpsimd.iota(blk_no[:, :], pattern=[[0, HC], [1, NB]], base=0, channel_multiplier=0,
                                 allow_small_or_imprecise_dtypes=True))
            const(nc.gpsimd.iota(tile_no[:, :], pattern=[[1, T]], base=0, channel_multiplier=0,
                                 allow_small_or_imprecise_dtypes=True))
            assert made == CONSTS

            def begin():
                pool.sem_inc(pool_begun, 1)

            at = bass.IndirectOffsetOnAxis

            def scatter_dst(slot, number):
                pool.wait_ge(staged, number)
                begin()
                for c in range(CH):
                    pool.indirect_dma_start(out=rec_dst, out_offset=at(ap=stage_pos[:, slot, c:c + 1], axis=0),
                                            in_=stage[:, slot, c, :], in_offset=None).then_inc(scattered[slot], 16)

            pool.wait_ge(rec_zero, 16 * 9)
            with pool.Fori(0, (NCH - 1) // 2) as i:
                for slot in range(2):
                    scatter_dst(slot, 2 * i + slot + 1)
            scatter_dst(0, NCH)
            pool.wait_ge(last_staged, 1)
            pool.indirect_dma_start(out=rec_dst, out_offset=at(ap=pos_dst[0:ER, EC:ECP], axis=0),
                                    in_=stage[0:ER, 1, 0, :], in_offset=None).then_inc(last_scattered, 16)

            def gather(g, source, index, width=D):
                for j in range(GT):
                    pool.indirect_dma_start(out=rows[:, g, j * D:(j + 1) * D], out_offset=None, in_=source,
                                            in_offset=at(ap=index(g, j), axis=0)).then_inc(gathered[g], 16)

            pool.wait_ge(table_out, 16)
            with pool.Fori(0, ROUNDS) as it:
                for g in range(SLOTS):
                    pool.wait_ge(rec_arrived[g], 16 * (it + 1))
                    pool.wait_ge(rows_free, (it * SLOTS + g + 1) * GT)
                    begin()
                    gather(g, table, lambda g, j: rec_in[:, g, j, 0:1])

            nc.gpsimd.iota(col_no, pattern=[[1, PC]], base=0, channel_multiplier=0,
                           allow_small_or_imprecise_dtypes=True).then_inc(col_no_made, 1)

            def gather_all(source, first):
                with pool.Fori(0, ROUNDS) as it:
                    for g in range(SLOTS):
                        pool.wait_ge(idx_in[g], (first - ROUNDS + it + 1) * 16)
                        begin()
                        gather(g, source, lambda g, j: idx_st[:, g, j:j + 1])
            for n, site in enumerate(("L1a", "L1b")):
                pool.wait_ge(table_out, 16 * (2 + n))
                gather_all(table, FIRST[site])
            for l, site in enumerate(("L2a", "L2b")):
                for j in range(2):
                    pool.wait_ge(rel_out[l][j], 16 * ((NB + 1 - j) // 2))
                gather_all(table_rel, FIRST[site])
            pool.wait_ge(flag_ready, 1)
            over_most = pool.value_load(flag[0:1, 0:1], min_val=0, max_val=1)
            with pool.If(over_most != 0):
                def scatter_src(slot, number):
                    pool.wait_ge(s_staged, number)
                    begin()
                    for c in range(CH):
                        pool.indirect_dma_start(out=rec_src, out_offset=at(ap=stage_pos[:, slot, c:c + 1], axis=0),
                                                in_=stage[:, slot, c, 0:SW], in_offset=None).then_inc(s_scattered[slot], 16)
                with pool.Fori(0, (NCH - 1) // 2) as i:
                    for slot in range(2):
                        scatter_src(slot, 2 * i + slot + 1)
                scatter_src(0, NCH)
                pool.wait_ge(last_staged, 2)
                pool.indirect_dma_start(out=rec_src, out_offset=at(ap=pos_src[0:ER, EC:ECP], axis=0),
                                        in_=stage[0:ER, 1, 0, 0:SW], in_offset=None).then_inc(last_scattered, 16)
                with pool.Fori(0, STEPS) as k:
                    pool.wait_ge(table_out, 16 * (k + 4))
                    begin()
                    gather_all(table, L3_FIRST + k * ROUNDS)

        @block.scalar
        def _(act):
            def std(number):
                act.wait_ge(std_in, number)
                nc.scalar.sqrt(rstd[:, :], rstd[:, :]).then_inc(std_out, 1)
            std(1)

            def put_together(slot, at_col, rnd, waits):
                act.wait_ge(ea_arrived[slot], 16 * rnd)
                if waits is not None:
                    act.wait_ge(scattered[slot], waits)
                nc.scalar.copy(stage[:, slot, :, 0:1], srow[:, bass.ds(at_col, CH)].unsqueeze(2))
                nc.scalar.copy(stage[:, slot, :, 1:2], rrow[:, bass.ds(at_col, CH)].unsqueeze(2))
                nc.scalar.copy(stage[:, slot, :, 2:3].bitcast(F32), dloc[:, bass.ds(at_col, CH)].unsqueeze(2))
                nc.scalar.copy(stage[:, slot, :, 3:4].bitcast(F32), sloc[:, bass.ds(at_col, CH)].unsqueeze(2))
                nc.scalar.copy(stage_pos[:, slot, :], pos_dst[:, bass.ds(at_col, CH)])
                nc.scalar.copy(stage[:, slot, :, 4:RW].bitcast(F32),
                               ea_in[:, slot, :].rearrange("p (c f) -> p c f", f=ED)).then_inc(staged, 1)

            act.wait_ge(pos_ready, 1)
            act.wait_ge(memset_done, 1)
            put_together(0, 0, 1, None)
            put_together(1, CH, 1, None)
            with act.Fori(0, (NCH - 3) // 2) as i:
                for slot in range(2):
                    put_together(slot, (2 * i + 2 + slot) * CH, i + 2, (i + 1) * (16 * CH))
            put_together(0, (NCH - 1) * CH, (NCH + 1) // 2, 16 * CH * ((NCH - 1) // 2))
            act.wait_ge(last_ea, 16)
            act.wait_ge(scattered[1], 16 * CH * ((NCH - 1) // 2))
            nc.scalar.copy(stage[0:ER, 1, 0, 0:1], srow[0:ER, EC:ECP])
            nc.scalar.copy(stage[0:ER, 1, 0, 1:2], rrow[0:ER, EC:ECP])
            nc.scalar.copy(stage[0:ER, 1, 0, 2:3].bitcast(F32), dloc[0:ER, EC:ECP])
            nc.scalar.copy(stage[0:ER, 1, 0, 3:4].bitcast(F32), sloc[0:ER, EC:ECP])
            nc.scalar.copy(stage[0:ER, 1, 0, 4:RW].bitcast(F32), ea_in[0:ER, 1, 0:ED]).then_inc(last_staged, 1)

            act.sem_inc(rec_free, SLOTS)
            act.sem_inc(eaT_sb, 1)
            with act.Fori(0, ROUNDS) as it:
                for g in range(SLOTS):
                    G = it * SLOTS + g
                    act.wait_ge(rec_arrived[g], 16 * (it + 1))
                    t0 = G * GT
                    nc.scalar.copy(ea_flat[:, :].rearrange("p (t f) -> p t f", t=GT),
                                   rec_in[:, g, :, 4:RW].bitcast(F32)).then_inc(ea_packed, 1)
                    nc.scalar.copy(row_src[:, bass.ds(t0, GT)], rec_in[:, g, :, 0])
                    nc.scalar.copy(row_rel[:, bass.ds(t0, GT)], rec_in[:, g, :, 1])
                    nc.scalar.copy(loc_dst[:, bass.ds(t0, GT)], rec_in[:, g, :, 2].bitcast(F32))
                    nc.scalar.copy(src_col[:, bass.ds(t0, GT)], rec_in[:, g, :, 3].bitcast(F32))
                    for half in range(2):
                        act.wait_ge(eaT_ps, 2 * G + half + 1)
                        nc.scalar.copy(eaT[:, :], tbank[0][:, 0:P]).then_inc(eaT_sb, 1)
                    act.wait_ge(pre_ready, G + 2)
                    nc.scalar.activation(rows[:, g, :], rows[:, g, :], ACT.Relu).then_inc(msg_ready, 1)

            def keep_transposed(n):
                for q in range(NT):
                    act.wait_ge(hT_ps[n], q + 1)
                    w = min(4, NB - 4 * q) * P
                    nc.scalar.copy(hT[:, q * BANK:q * BANK + w], tbank[q % 2][0:D, 0:w]).then_inc(hT_sb[n], 1)

            keep_transposed(0)
            for q in range(NT):
                w = min(4, NB - 4 * q) * P
                at_q = slice(q * BANK, q * BANK + w)
                act.wait_ge(mlp_ps, q + 1)
                nc.scalar.activation(hT[:, at_q], part[q % 2][0:D, 0:w], ACT.Relu, bias=cols[:, 0:1]).then_inc(mlp_hid, 1)
                act.wait_ge(mlp_ps2, q + 1)
                nc.scalar.activation(hT[:, at_q], part[2 + q % 2][0:D, 0:w], ACT.Identity, bias=cols[:, 1:2]).then_inc(mlp_out, 1)
            act.wait_ge(bn_in, 1)
            nc.scalar.sqrt(bcol[:, 0:1], bcol[:, 0:1]).then_inc(bn_std, 1)
            act.wait_ge(bn_ready, 1)
            for q in range(NT):
                w = min(4, NB - 4 * q) * P
                at_q = slice(q * BANK, q * BANK + w)
                nc.scalar.activation(hT[:, at_q], hT[:, at_q], ACT.Relu, bias=bcol[:, 2:3],
                                     scale=bcol[:, 1:2]).then_inc(bn_out, 1)

            act.wait_ge(t_pre, 1)
            nc.scalar.activation(t_sig[:, :], t_row[:, :], ACT.Sigmoid).then_inc(t_act, 1)
            act.wait_ge(root_in, 1)
            nc.scalar.sqrt(factors[:, :, :], factors[:, :, :]).then_inc(root_out, 1)
            std(2)

            for f in range(4):
                act.sem_inc(counts_out[f], 16)
            act.sem_inc(checked, 1)

            def keep_sums(first, tiles):
                with act.Fori(0, ROUNDS) as it:
                    for g in range(SLOTS):
                        of, after = blocks_of(act, tiles, it * (SLOTS * GT) + g * GT)
                        of = of + after
                        for j in range(GT):
                            n = (first + it) * (SLOTS * GT) + g * GT + j
                            with act.If(of[j + 1] != of[j + 2]):
                                act.wait_ge(rows_free, n + SLOTS * GT + 1)
                                act.sem_inc(act_begun, 1)
                                nc.scalar.copy(acc[:, bass.ds(of[j + 1] * D, D)], summed).then_inc(kept, 1)
                                act.wait_ge(kept, n + 2)
                                act.sem_inc(act_begun, 1)
                            with act.Else():
                                act.sem_inc(kept, 1)

            def keep_counts(first, f):
                groups = min(PG, SG - f * PG)
                with act.Fori(0, ROUNDS) as it:
                    for g in range(SLOTS):
                        t0 = it * (SLOTS * GT) + g * GT
                        of, after = blocks_of(act, tiles_dst, t0)
                        of = of + after
                        for j in range(GT):
                            t, n, b = t0 + j, t0 + j + f * T, of[j + 1]
                            with act.If(b != of[j + 2]):
                                act.wait_ge(oh_free, n + RING + 1)
                                act.wait_ge(checked, n + 1)
                                act.sem_inc(act_begun, 1)
                                nc.scalar.copy(acc[:, bass.ds(b * D, D)], summed)
                                for i in range(2 * groups):
                                    last = nc.scalar.copy(whole_counts[:, i * HALF:(i + 1) * HALF], wide[i][:, 0:HALF])
                                last.then_inc(kept, 1)
                                act.wait_ge(kept, (first + it) * (SLOTS * GT) + g * GT + j + 2)
                                act.wait_ge(counts_out[f], (t + 1) * 16)
                                act.sem_inc(act_begun, 1)
                                nc.scalar.copy(counted[:, 0:groups * GC], whole_counts[:, 0:groups * GC],
                                               saturate=False).then_inc(packed, 1)
                                act.wait_ge(packed, n + 1)
                                to = counts[f * PG:f * PG + groups, :, bass.ds(b * GC, GC)]
                                act.dma_start(to.rearrange("g p c -> p g c"),
                                              counted[:, 0:groups * GC].bitcast(U8).rearrange("p (g c) -> p g c", g=groups)
                                              ).then_inc(counts_out[f], 16)
                                nc.scalar.activation(over_out[:, 0:groups * GC], whole_counts[:, 0:groups * GC],
                                                     ACT.Relu, bias=minus[:, 0:1],
                                                     accum_out=over[:, bass.ds(b * 4 + f, 1)]).then_inc(checked, 1)
                            with act.Else():
                                act.sem_inc(kept, 1)
                                act.sem_inc(packed, 1)
                                act.sem_inc(counts_out[f], 16)
                                act.sem_inc(checked, 1)
                act.wait_ge(counts_out[f], 16 * (T + 1))
                act.wait_ge(checked, (f + 1) * T + 1)

            keep_transposed(1)
            keep_counts(FIRST["L1a"], 0)
            keep_transposed(2)
            keep_counts(FIRST["L1b"], 1)
            act.wait_ge(silu_in, 1)
            nc.scalar.activation(acc[:, :], tab[:, :], ACT.Sigmoid).then_inc(silu_out, 1)
            std(3)
            for l, site in enumerate(("L2a", "L2b")):
                keep_transposed(3 + l)
                for b in range(NB):
                    act.wait_ge(rel_ps[l], b + 1)
                    if b >= 2:
                        act.wait_ge(rel_out[l][b % 2], 16 * (b // 2))
                    lo = (tbank if b % 2 else pbank)[0]
                    nc.scalar.copy(rel_st[:, b % 2, 0:4 * D], lo[:, 0:4 * D]).then_inc(rel_a[l], 1)
                keep_counts(FIRST[site], 2 + l)
            std(4)
            act.wait_ge(flag_ready, 1)
            over_most = act.value_load(flag[0:1, 0:1], min_val=0, max_val=1)
            with act.If(over_most == 0):
                act.sem_inc(bank_free, SB)
                with act.Fori(0, STEPS) as k:
                    with act.Fori(0, SG) as g:
                        n = k * SG + g
                        act.wait_ge(sums_used, n + 1)
                        for j in range(SB):
                            act.wait_ge(bank_done, n * SB + SB + j + 1)
                            nc.scalar.copy(sums[:, j, :], banks[j][:, 0:2 * D]).then_inc(bank_free, 1)
            with act.Else():
                def put_src(slot, at_col, waits):
                    if waits is not None:
                        act.wait_ge(s_scattered[slot], waits)
                    nc.scalar.copy(stage[:, slot, :, 0:1], drow[:, bass.ds(at_col, CH)].unsqueeze(2))
                    nc.scalar.copy(stage[:, slot, :, 1:2].bitcast(F32), sloc[:, bass.ds(at_col, CH)].unsqueeze(2))
                    nc.scalar.copy(stage_pos[:, slot, :], pos_src[:, bass.ds(at_col, CH)]).then_inc(s_staged, 1)
                act.wait_ge(pos_ready, 2)
                put_src(0, 0, None)
                put_src(1, CH, None)
                with act.Fori(0, (NCH - 3) // 2) as i:
                    for slot in range(2):
                        put_src(slot, (2 * i + 2 + slot) * CH, (i + 1) * (16 * CH))
                put_src(0, (NCH - 1) * CH, 16 * CH * ((NCH - 1) // 2))
                act.wait_ge(s_scattered[1], 16 * CH * ((NCH - 1) // 2))
                nc.scalar.copy(stage[0:ER, 1, 0, 0:1], drow[0:ER, EC:ECP])
                nc.scalar.copy(stage[0:ER, 1, 0, 1:2].bitcast(F32), sloc[0:ER, EC:ECP]).then_inc(last_staged, 1)
                with act.Fori(0, STEPS) as k:
                    keep_sums(L3_FIRST + k * ROUNDS, tiles_src)

        @block.tensor
        def _(pe):
            pe.sem_inc(rows_free, SLOTS * GT)
            pe.wait_ge(consts, CONSTS)
            for k in range(2):
                pe.wait_ge(cnt_ready, k + 1)
                nc.tensor.matmul(pbank[0][:, 0:NB], ones[:, :], cnt[:, :], start=True, stop=True)
                nc.tensor.matmul(pbank[1][:, 0:NB], before[:, :], cnt[:, :], start=True, stop=True)
                nc.tensor.matmul(tbank[0][0:NB, 0:1], cnt[:, :], ones[:, 0:1], start=True, stop=True).then_inc(tot_ready, 1)
                pe.wait_ge(tilesT_ready, k + 1)
                nc.tensor.matmul(tbank[1][0:NB, 0:1], upto[:, :], totT[:, :], start=True, stop=True).then_inc(endT_ready, 1)
                pe.wait_ge(ge_ready, k + 1)
                for half in range(2):
                    last = nc.tensor.matmul(part[half][0:1, 0:T // 2], ones[0:NB, 0:1],
                                            tile_ge[:, half * (T // 2):(half + 1) * (T // 2)], start=True, stop=True)
                last.then_inc(off_ready, 1)
            for k in range(2):
                hist = pbank[k][:, 0:NB]

                def count(slot, number, columns, start=False, stop=False):
                    pe.wait_ge(hist_ready, number)
                    for c in range(columns):
                        last = nc.tensor.matmul(hist, oh_loc[:, slot, c, :], oh_blk[:, slot, c, :],
                                                start=start and c == 0, stop=stop)
                    last.then_inc(hist_used, 1)
                count(0, (HS + 1) * k + 1, HC, start=True)
                with pe.Fori(0, HS // 2) as i:
                    for s in range(2):
                        count(1 - s, (HS + 1) * k + 2 + 2 * i + s, HC)
                count(1, (HS + 1) * (k + 1), 1, stop=True)

            def sum_tiles(g, G, tiles, t0, f=None):
                of, _ = blocks_of(pe, tiles, t0)
                halves = 0 if f is None else 2 * min(PG, SG - f * PG)
                pe.wait_ge(onehot_ready, G + 1)

                def products(j, first):
                    nc.tensor.matmul(summed, onehot[:, g % 2, j * P:(j + 1) * P], rows[:, g, j * D:(j + 1) * D],
                                     start=first, stop=True, skip_group_check=True).then_inc(rows_free, 1)
                    for i in range(halves):
                        last = nc.tensor.matmul(wide[i][:, 0:HALF], rows_oh[j % RING],
                                                cols_oh[j % RING][:, i * HALF:(i + 1) * HALF], start=first,
                                                stop=True, skip_group_check=True)
                    if halves:
                        last.then_inc(oh_free, 1)
                for j in range(GT):
                    if halves:
                        pe.wait_ge(oh_ready, t0 + j + f * T + 1)
                    with pe.If(of[j + 1] != of[j]):
                        pe.wait_ge(kept, G * GT + j + 1)
                        products(j, True)
                    with pe.Else():
                        products(j, False)

            pe.wait_ge(weights_in, 16 * WEIGHTS)
            pe.wait_ge(hist_out, 1)
            pe.wait_ge(tiles_known, 1)
            with pe.Fori(0, ROUNDS) as it:
                for g in range(SLOTS):
                    G = it * SLOTS + g
                    pe.wait_ge(ea_packed, G + 1)
                    for half in range(2):
                        pe.wait_ge(eaT_sb, 2 * G + half + 1)
                        nc.tensor.transpose(tbank[0][:, 0:P], ea_flat[:, half * P:(half + 1) * P],
                                            ident[:, :]).then_inc(eaT_ps, 1)
                        pe.wait_ge(eaT_sb, 2 * G + half + 2)
                        pe.wait_ge(pre_ready, G + 1)
                        last = nc.tensor.matmul(pbank[half][:, 0:4 * D], eaT[:, :], we_diag[:, :], start=True, stop=True)
                    last.then_inc(eaw_ready, 1)
                    pe.wait_ge(msg_ready, G + 1)
                    sum_tiles(g, G, tiles_dst, G * GT)

            def transpose_nodes(n, a):
                pe.wait_ge(hT_in[n], 1)
                for q in range(NT):
                    if q >= 2:
                        pe.wait_ge(hT_sb[n], q - 1)
                    for b in range(4 * q, min(NB, 4 * q + 4)):
                        last = nc.tensor.transpose(tbank[q % 2][0:D, (b - 4 * q) * P:(b - 4 * q + 1) * P],
                                                   a[:, b * D:(b + 1) * D], ident[:, :])
                    last.then_inc(hT_ps[n], 1)

            transpose_nodes(0, h)
            for q in range(NT):
                w = min(4, NB - 4 * q) * P
                at_q = slice(q * BANK, q * BANK + w)
                pe.wait_ge(hT_sb[0], NT)
                if q >= 2:
                    pe.wait_ge(mlp_out, q - 1)
                nc.tensor.matmul(part[q % 2][0:D, 0:w], w1a[:, :], hT[:, at_q], start=True, stop=True).then_inc(mlp_ps, 1)
                pe.wait_ge(mlp_hid, q + 1)
                nc.tensor.matmul(part[2 + q % 2][0:D, 0:w], w2a[:, :], hT[:, at_q], start=True, stop=True).then_inc(mlp_ps2, 1)
            for q in range(NQ):
                pe.wait_ge(bn_out, min(NT, -(-((q + 1) * CB) // 4)))
                if q >= 2:
                    pe.wait_ge(back_used, q - 1)
                for b in range(CB * q, min(NB, CB * q + CB)):
                    last = nc.tensor.transpose(pbank[q % 2][:, (b - CB * q) * D:(b - CB * q + 1) * D],
                                               hT[:, b * P:(b + 1) * P], ident[0:D, 0:D])
                last.then_inc(back_ps, 1)

            pe.wait_ge(back_used, NQ)
            for c in range(3):
                last = nc.tensor.matmul(pbank[0][:, 0:D], t_rep[:, c, :], we1[:, c, :], start=(c == 0), stop=(c == 2))
            last.then_inc(t_ps, 1)

            def project(n, w_, tn):
                for q in range(NQ):
                    pe.wait_ge(hT_sb[tn], NT)
                    if q >= 2:
                        pe.wait_ge(proj_used[n], q - 1)
                    for b in range(CB * q, min(NB, CB * q + CB)):
                        last = nc.tensor.matmul(pbank[q % 2][:, (b - CB * q) * D:(b - CB * q + 1) * D],
                                                hT[:, b * P:(b + 1) * P], w_[:, :], start=True, stop=True)
                    last.then_inc(proj_ps[n], 1)

            def sum_edges(first, tiles, f=None):
                with pe.Fori(0, ROUNDS) as it:
                    for g in range(SLOTS):
                        pe.wait_ge(gathered[g], (first + it + 1) * (16 * GT))
                        sum_tiles(g, (first + it) * SLOTS + g, tiles, it * (SLOTS * GT) + g * GT, f)
                pe.wait_ge(kept, (first + ROUNDS) * (SLOTS * GT) + 1)

            transpose_nodes(1, h)
            pe.wait_ge(t_pre, 1)
            project(0, w1b, 1)
            pe.wait_ge(proj_used[0], NQ)
            sum_edges(FIRST["L1a"], tiles_dst, 0)
            transpose_nodes(2, acc)
            project(1, w2b, 2)
            pe.wait_ge(proj_used[1], NQ)
            sum_edges(FIRST["L1b"], tiles_dst, 1)
            for l, site in enumerate(("L2a", "L2b")):
                transpose_nodes(3 + l, h)
                project(2 + l, lw[l], 3 + l)
                pe.wait_ge(proj_used[2 + l], NQ)
                for b in range(NB):
                    if b >= 2:
                        pe.wait_ge(rel_a[l], b - 1)
                        pe.wait_ge(rel_b[l], b - 1)
                    pair = tbank if b % 2 else pbank
                    for half in range(2):
                        last = nc.tensor.matmul(pair[half][:, 0:4 * D], hT[:, b * P:(b + 1) * P],
                                                rw[l][:, half * 4 * D:(half + 1) * 4 * D], start=True, stop=True)
                    last.then_inc(rel_ps[l], 1)
                pe.wait_ge(rel_a[l], NB)
                pe.wait_ge(rel_b[l], NB)
                sum_edges(FIRST[site], tiles_dst, 2 + l)

            pe.wait_ge(most_ready, 1)
            nc.tensor.matmul(banks[6][0:1, 0:1], most[:, :], ones[:, 0:1], start=True, stop=True).then_inc(most_ps, 1)
            pe.wait_ge(flag_ready, 1)
            over_most = pe.value_load(flag[0:1, 0:1], min_val=0, max_val=1)
            with pe.If(over_most == 0):
                pe.sem_inc(slot_free, SG - 1)
                pe.sem_inc(bank_done, SB)
                with pe.Fori(0, STEPS) as k:
                    with pe.Fori(0, SG) as g:
                        n = k * SG + g
                        for c in range(SG):
                            pe.wait_ge(z_ready, k * SG + c + 1)
                            pe.wait_ge(counts_in[c], (n + 1) * 16)
                            for j in range(SB):
                                if c == 0:
                                    pe.wait_ge(bank_free, n * SB + j + 1)
                                if c == 0 or j == 0:
                                    pe.sem_inc(pe_begun, 1)
                                for i in range(SB):
                                    last = nc.tensor.matmul(banks[j][:, 0:2 * D],
                                                            slots[c][:, i * GC + j * P:i * GC + (j + 1) * P],
                                                            z[:, c * SB + i, :], start=(c == 0 and i == 0),
                                                            stop=(c == SG - 1 and i == SB - 1))
                                if c == SG - 1:
                                    last.then_inc(bank_done, 1)
                            if c < SG - 1:
                                last.then_inc(slot_free, 1)
            with pe.Else():
                with pe.Fori(0, STEPS) as k:
                    sum_edges(L3_FIRST + k * ROUNDS, tiles_src)

        @block.vector
        def _(dve):
            chain = Count(dve_step)

            def then(ins):
                chain.step(ins)
                dve.wait_ge(chain.sem, chain.value)

            V = nc.vector
            V.memset(xs[:, (NB - 1) * D:W], 0.0)
            V.memset(we_diag[:, :], 0.0)
            V.memset(minus[:, :], -float(MOST))
            V.memset(over[:, :], 0.0)
            V.memset(rw[0][:, :], 0.0)
            V.memset(rw[1][:, :], 0.0)
            V.memset(stage[:, :, :, :].bitcast(F32).rearrange("p s c w -> p (s c w)"), 0.0)
            V.memset(acc[:, :], 0.0).then_inc(memset_done, 1)
            dve.sem_inc(kept, 1)
            dve.sem_inc(pre_ready, 1)

            def norm(number, relu_to):
                for b in range(NB):
                    V.bn_stats(stats[:, b, :], xs[:, b * D:(b + 1) * D]).then_inc(dve_step, 1)
                chain.value = chain.value + NB
                dve.wait_ge(dve_step, chain.value)
                for b in range(NB):
                    V.bn_aggr(mv[:, b, :], stats[:, b, :]).then_inc(dve_step, 1)
                chain.value = chain.value + NB
                dve.wait_ge(dve_step, chain.value)
                V.tensor_scalar(rstd[:, :], mv[:, :, 1], 1e-5, None, ALU.add).then_inc(std_in, 1)
                then(V.tensor_tensor(blocks(relu_to), blocks(xs), by_node(mv[:, :, 0]), ALU.subtract))
                dve.wait_ge(std_out, number)
                then(V.reciprocal(rstd[:, :], rstd[:, :]))
                then(V.tensor_tensor(blocks(relu_to), blocks(relu_to), by_node(rstd), ALU.mult))
                then(V.tensor_scalar(relu_to[:, :], relu_to[:, :], 0.0, None, ALU.max))

            dve.wait_ge(x_in, 32)
            norm(1, h)
            dve.wait_ge(weights_in, 16 * WEIGHTS)
            for c in range(3):
                then(V.tensor_copy(t_rep[:, c, :], t_col[:, c:c + 1].broadcast_to([P, P])))

            dve.wait_ge(edges_in, 16 * 6)
            dve.wait_ge(memset_done, 1)
            for key, loc, row in (("src", sloc, srow), ("dst", dloc, drow)):
                then(V.memset(blk[key][:, EC:ECP], 2.0 * NB))
                then(V.memset(loc[:, EC:ECP], 0.0))
                for lo, hi, n in ((0, EC, P), (EC, ECP, ER)):
                    a = ints[key][0:n, lo:hi]
                    then(V.tensor_scalar(low[0:n, lo:hi], a, P - 1, None, ALU.bitwise_and))
                    then(V.tensor_scalar(high[0:n, lo:hi], a, 7, None, ALU.logical_shift_right))
                    then(V.tensor_copy(blk[key][0:n, lo:hi], high[0:n, lo:hi]))
                    then(V.tensor_scalar(loc[0:n, lo:hi], low[0:n, lo:hi], 1.0, None, ALU.add))
                    then(V.scalar_tensor_tensor(row[0:n, lo:hi], low[0:n, lo:hi], float(NB), high[0:n, lo:hi],
                                                ALU.mult, ALU.add))
            for lo, hi, n in ((0, EC, P), (EC, ECP, ER)):
                then(V.scalar_tensor_tensor(rrow[0:n, lo:hi], srow[0:n, lo:hi], float(RELS),
                                            ints["type"][0:n, lo:hi], ALU.mult, ALU.add))

            dve.wait_ge(consts, CONSTS)

            def sort(k, key, pos, tiles):
                for b in range(NB):
                    then(V.tensor_scalar(cum, blk[key], float(b), 0.0, ALU.is_equal, ALU.add,
                                         accum_out=cnt[:, b:b + 1]))
                dve.sem_inc(cnt_ready, 1)
                dve.wait_ge(tot_ready, k + 1)
                then(V.tensor_scalar(totT_i[:, :], tbank[0][0:NB, 0:1], float(P - 1), None, ALU.add))
                then(V.tensor_scalar(totT_i[:, :], totT_i[:, :], 7, None, ALU.logical_shift_right))
                then(V.tensor_scalar(totT[:, :], totT_i[:, :], 1.0, None, ALU.max))
                dve.sem_inc(tilesT_ready, 1)
                then(V.tensor_scalar(tot_i[:, :], pbank[0][:, 0:NB], float(P - 1), None, ALU.add))
                then(V.tensor_scalar(tot_i[:, :], tot_i[:, :], 7, None, ALU.logical_shift_right))
                then(V.tensor_scalar(tot[:, :], tot_i[:, :], 1.0, None, ALU.max))
                then(V.tensor_tensor_scan(ends[:, :], tot[:, :], acc[:, 0:NB], 0.0, ALU.add, ALU.add))
                then(V.tensor_tensor(start[:, :], ends[:, :], tot[:, :], ALU.subtract))
                then(V.scalar_tensor_tensor(start[:, :], start[:, :], float(P), pbank[1][:, 0:NB], ALU.mult, ALU.add))
                then(V.tensor_scalar(start[:, :], start[:, :], -1.0, None, ALU.add))
                dve.wait_ge(endT_ready, k + 1)
                then(V.tensor_copy(endT[:, :], tbank[1][0:NB, 0:1]))
                then(V.tensor_scalar(tile_ge[:, :], tile_no[:, :], endT[:, 0:1], None, ALU.is_ge))
                dve.sem_inc(ge_ready, 1)
                dve.wait_ge(off_ready, k + 1)
                then(V.memset(tiles[:, :].bitcast(F32), 0.0))
                then(V.tensor_scalar(tiles[:, :], tiles[:, :], float(NB), None, ALU.add))
                for half in range(2):
                    lo = PADT + half * (T // 2)
                    then(V.tensor_scalar(tiles[0:1, lo:lo + T // 2], part[half][0:1, 0:T // 2], float(NB - 1), None, ALU.min))
                for b in range(NB):
                    then(V.tensor_scalar(eq, blk[key], float(b), None, ALU.is_equal))
                    then(V.tensor_tensor_scan(cum, eq, zero_row, start[:, b:b + 1], ALU.add, ALU.add))
                    then(V.copy_predicated(pos_f, eq, cum))
                then(V.tensor_copy(low, pos_f))
                then(V.tensor_scalar(high, low, 7, None, ALU.logical_shift_right))
                then(V.tensor_scalar(low, low, P - 1, None, ALU.bitwise_and))
                V.scalar_tensor_tensor(pos[:, :], low, float(T), high, ALU.mult, ALU.add).then_inc(pos_ready, 1)
                dve.wait_ge(pos_ready, k + 1)

            then(V.memset(pos_f, 0.0))
            sort(0, "dst", pos_dst, tiles_dst)
            sort(1, "src", pos_src, tiles_src)
            dve.sem_inc(tiles_known, 1)

            def hist(k, key, loc):
                def make(slot, c0, n, used):
                    if used is not None:
                        dve.wait_ge(hist_used, used)
                    lc = places[:, 0:P].unsqueeze(1).broadcast_to([P, n, P])
                    bc = blk_no[:, 0:n * NB].rearrange("p (c b) -> p c b", c=n)
                    V.tensor_tensor(oh_loc[:, slot, 0:n, :], lc,
                                    loc[:, bass.ds(c0, n)].unsqueeze(2).broadcast_to([P, n, P]), ALU.is_equal)
                    V.tensor_tensor(oh_blk[:, slot, 0:n, :], bc,
                                    blk[key][:, bass.ds(c0, n)].unsqueeze(2).broadcast_to([P, n, NB]),
                                    ALU.is_equal).then_inc(hist_ready, 1)
                done = (HS + 1) * k
                make(0, 0, HC, done if k else None)
                make(1, HC, HC, None)
                make(0, 2 * HC, HC, done + 1)
                with dve.Fori(0, HS // 2 - 1) as i:
                    for s in range(2):
                        make(1 - s, (2 * i + s + 3) * HC, HC, done + 2 * i + s + 2)
                make(1, EC, 1, done + HS - 1)
            hist(0, "dst", dloc)
            hist(1, "src", sloc)
            dve.wait_ge(hist_used, 2 * (HS + 1))
            then(V.tensor_copy(deg["dst"][:, :], pbank[0][:, 0:NB]))
            then(V.tensor_copy(deg["src"][:, :], pbank[1][:, 0:NB]))
            dve.sem_inc(hist_out, 1)
            V.tensor_tensor(blocks(tab), blocks(h), by_feature(be_row[:, :], NB), ALU.add).then_inc(table_ready, 1)

            def make_onehot(g, G, places_of):
                dve.wait_ge(rows_free, (G + SLOTS - 1) * GT)
                V.tensor_tensor(onehot[:, g % 2, :].rearrange("p (t n) -> p t n", t=GT),
                                places[:, :].rearrange("p (t n) -> p t n", t=GT),
                                places_of.unsqueeze(2).broadcast_to([P, GT, P]), ALU.is_equal).then_inc(onehot_ready, 1)

            with dve.Fori(0, ROUNDS) as it:
                for g in range(SLOTS):
                    G = it * SLOTS + g
                    dve.wait_ge(rec_arrived[g], 16 * (it + 1))
                    make_onehot(g, G, rec_in[:, g, :, 2].bitcast(F32))
                    of, after = blocks_of(dve, tiles_dst, G * GT)
                    of = of + after
                    dve.wait_ge(gathered[g], (it + 1) * (16 * GT))
                    dve.wait_ge(eaw_ready, G + 1)
                    for half in range(2):
                        a = rows[:, g, half * 4 * D:(half + 1) * 4 * D]
                        last = V.tensor_tensor(a, a, pbank[half][:, 0:4 * D], ALU.add)
                    last.then_inc(pre_ready, 1)
                    for j in range(GT):
                        n = G * GT + j
                        with dve.If(of[j + 1] != of[j + 2]):
                            dve.wait_ge(rows_free, n + SLOTS * GT + 1)
                            V.tensor_copy(acc[:, bass.ds(of[j + 1] * D, D)], summed).then_inc(kept, 1)
                            dve.wait_ge(kept, n + 2)
                            dve.sem_inc(dve_begun, 1)
                        with dve.Else():
                            dve.sem_inc(kept, 1)
                    dve.wait_ge(msg_ready, G + 1)
                    dve.sem_inc(rec_free, 1)
            dve.wait_ge(kept, T + 1)

            def count_onehots(f, t0):
                width = min(PG, SG - f * PG) * GC
                for j in range(GT):
                    n = t0 + j + f * T
                    dve.wait_ge(oh_free, n + 1)
                    V.tensor_scalar(cols_oh[j % RING][:, 0:width], col_no[:, 0:width], src_col[:, bass.ds(t0 + j, 1)], None,
                                    ALU.is_equal)
                    V.tensor_scalar(rows_oh[j % RING], place_no[:, :], loc_dst[:, bass.ds(t0 + j, 1)], None,
                                    ALU.is_equal).then_inc(oh_ready, 1)

            def sum_edges(first, places_of, f=None):
                with dve.Fori(0, ROUNDS) as it:
                    for g in range(SLOTS):
                        t0 = it * (SLOTS * GT) + g * GT
                        make_onehot(g, (first + it) * SLOTS + g, places_of(t0))
                        if f is not None:
                            count_onehots(f, t0)
                dve.wait_ge(kept, (first + ROUNDS) * (SLOTS * GT) + 1)
                if f is not None:
                    dve.wait_ge(oh_free, (f + 1) * T + RING)
                    then(V.tensor_scalar(src_col[:, :], src_col[:, :], -float(PC), None, ALU.add))

            V.tensor_tensor(h[:, :], h[:, :], acc[:, :], ALU.add).then_inc(hT_in[0], 1)
            for q in range(NT):
                w = min(P * 4, N - q * BANK)
                dve.wait_ge(mlp_out, q + 1)
                V.bn_stats(bstats[:, q, :], hT[:, q * BANK:q * BANK + w]).then_inc(dve_step, 1)
            chain.value = chain.value + NT
            dve.wait_ge(dve_step, chain.value)
            then(V.bn_aggr(bmv[:, :], bstats[:, :, :].rearrange("p q s -> p (q s)")))
            V.tensor_scalar(bcol[:, 0:1], bmv[:, 1:2], 1e-5, None, ALU.add).then_inc(bn_in, 1)
            dve.wait_ge(bn_std, 1)
            then(V.reciprocal(bcol[:, 3:4], bcol[:, 0:1]))
            then(V.tensor_tensor(bcol[:, 1:2], bcol[:, 3:4], cols[:, 2:3], ALU.mult))
            then(V.tensor_tensor(bcol[:, 3:4], bmv[:, 0:1], bcol[:, 1:2], ALU.mult))
            V.tensor_tensor(bcol[:, 2:3], cols[:, 3:4], bcol[:, 3:4], ALU.subtract).then_inc(bn_ready, 1)
            for q in range(NQ):
                n = min(CB, NB - CB * q)
                dve.wait_ge(back_ps, q + 1)
                a = blocks(xs, q)
                V.tensor_tensor(a, a, pbank[q % 2][:, 0:n * D].rearrange("p (b f) -> p b f", f=D), ALU.add).then_inc(back_used, 1)
            dve.wait_ge(back_used, NQ)

            then(V.tensor_scalar(src_col[:, :], src_col[:, :], -1.0, -float(P * NB - 1), ALU.add, ALU.mult))
            then(V.scalar_tensor_tensor(src_col[:, :], row_src, float(P), src_col[:, :], ALU.mult, ALU.add))
            then(V.tensor_copy(place_no[:, :], places[:, 0:P]))
            dve.wait_ge(col_no_made, 1)
            dve.sem_inc(oh_free, RING)

            then(V.tensor_scalar(dinv, deg["dst"][:, :], 1.0, None, ALU.add))
            then(V.tensor_scalar(norm2[:, :], deg["dst"][:, :], 1.0, None, ALU.max))
            then(V.tensor_scalar(w_row, deg["src"][:, :], 1.0, None, ALU.max))
            then(V.tensor_copy(w_col, norm2[:, :]))
            then(V.reciprocal(norm2[:, :], norm2[:, :]))
            dve.wait_ge(t_ps, 1)
            then(V.tensor_tensor(t_row[:, :], pbank[0][:, 0:D], be1_row[:, :], ALU.add))
            dve.sem_inc(t_pre, 1)
            dve.wait_ge(t_act, 1)
            then(V.tensor_tensor(t_row[:, :], t_row[:, :], t_sig[:, :], ALU.mult))
            then(V.tensor_tensor(b1_row[:, :], b1_row[:, :], t_row[:, :], ALU.add))
            dve.sem_inc(root_in, 1)
            dve.wait_ge(root_out, 1)
            then(V.reciprocal(factors[:, :, :], factors[:, :, :]))
            norm(2, h)
            dve.sem_inc(hT_in[1], 1)

            def projected(n, scale, row):
                for q in range(NQ):
                    m = min(CB, NB - CB * q)
                    dve.wait_ge(proj_ps[n], q + 1)
                    p = pbank[q % 2][:, 0:m * D].rearrange("p (b f) -> p b f", f=D)
                    if scale is not None:
                        V.tensor_tensor(blocks(tab, q), p, by_node(scale, CB * q, CB * q + m), ALU.mult).then_inc(proj_used[n], 1)
                    else:
                        V.tensor_tensor(blocks(tab, q), p, by_feature(row, m), ALU.add).then_inc(proj_used[n], 1)
                dve.wait_ge(proj_used[n], NQ)

            for n, row in ((0, b1_row), (1, b2_row)):
                projected(n, dinv, None)
                dve.sem_inc(table_ready, 1)
                sum_edges(FIRST["L1a" if n == 0 else "L1b"], lambda t: loc_dst[:, bass.ds(t, GT)], n)
                to = tab if n else acc
                then(V.tensor_tensor(acc[:, :], acc[:, :], tab[:, :], ALU.add))
                then(V.tensor_tensor(blocks(acc), blocks(acc), by_node(dinv), ALU.mult))
                then(V.tensor_tensor(blocks(to), blocks(acc), by_feature(row[:, :], NB), ALU.add))
                dve.sem_inc(silu_in if n else hT_in[2], 1)
            dve.wait_ge(silu_out, 1)
            then(V.tensor_tensor(tab[:, :], tab[:, :], acc[:, :], ALU.mult))
            then(V.tensor_tensor(tab[:, :], tab[:, :], h[:, :], ALU.add))
            then(V.tensor_tensor(xs[:, :], xs[:, :], tab[:, :], ALU.add))
            norm(3, h)
            for l, site in enumerate(("L2a", "L2b")):
                dve.sem_inc(hT_in[3 + l], 1)
                projected(2 + l, None, bias2[:, l, :])
                for b in range(NB):
                    dve.wait_ge(rel_ps[l], b + 1)
                    if b >= 2:
                        dve.wait_ge(rel_out[l][b % 2], 16 * (b // 2))
                    hi = (tbank if b % 2 else pbank)[1]
                    V.tensor_copy(rel_st[:, b % 2, 4 * D:8 * D], hi[:, 0:4 * D]).then_inc(rel_b[l], 1)
                sum_edges(FIRST[site], lambda t: loc_dst[:, bass.ds(t, GT)], 2 + l)
                then(V.tensor_tensor(blocks(acc), blocks(acc), by_node(norm2), ALU.mult))
                then(V.tensor_tensor(acc[:, :], acc[:, :], tab[:, :], ALU.add))
                if l == 0:
                    then(V.tensor_scalar(h[:, :], acc[:, :], 0.0, None, ALU.max))
                else:
                    then(V.tensor_tensor(xs[:, :], xs[:, :], acc[:, :], ALU.add))
            norm(4, h)
            dve.wait_ge(checked, 4 * T + 1)
            then(V.tensor_reduce(most[:, :], over[:, :], X, ALU.max))
            then(V.tensor_scalar(most[:, :], most[:, :], 1.0, None, ALU.min))
            dve.sem_inc(most_ready, 1)
            dve.wait_ge(most_ps, 1)
            then(V.tensor_scalar(flag[:, :], banks[6][0:1, 0:1], 0.0, None, ALU.is_gt))
            dve.sem_inc(flag_ready, 1)
            over_most = dve.value_load(flag[0:1, 0:1], min_val=0, max_val=1)
            with dve.If(over_most == 0):
                chain = Count(dense_step)
                then(V.tensor_tensor(f1[:, :], w_row, w_col, ALU.mult))
                then(V.tensor_scalar(f1[:, :], f1[:, :], BETA, None, ALU.mult))
                then(V.tensor_scalar(f2[:, :], w_col, ZS * THETA, None, ALU.mult))
                then(V.reciprocal(f2[:, :], f2[:, :]))
                then(V.tensor_tensor(blocks(acc), blocks(h), by_node(w_col), ALU.mult))
                then(V.tensor_scalar(acc[:, :], acc[:, :], ZS, None, ALU.mult))

                def split(c):
                    a = blocks(acc)[:, c * SB:(c + 1) * SB, :]
                    zc = z[:, c * SB:(c + 1) * SB, :]
                    then(V.tensor_copy(zc[:, :, 0:D], a))
                    V.tensor_tensor(zc[:, :, D:2 * D], a, zc[:, :, 0:D], ALU.subtract).then_inc(z_ready, 1)

                def finish(n, g):
                    dve.wait_ge(bank_free, n * SB + 2 * SB)
                    t3 = total.rearrange("p (b f) -> p b f", f=D)
                    then(V.tensor_tensor(t3, sums[:, :, 0:D], sums[:, :, D:2 * D], ALU.add))
                    dve.sem_inc(sums_used, 1)
                    then(V.tensor_tensor(t3, t3, f1[:, bass.ds(g * SB, SB)].unsqueeze(2).broadcast_to([P, SB, D]), ALU.mult))
                    then(V.tensor_tensor(acc[:, bass.ds(g * (SB * D), SB * D)], total,
                                         h[:, bass.ds(g * (SB * D), SB * D)], ALU.add))

                for c in range(SG):
                    split(c)
                then(V.tensor_scalar(h[:, :], acc[:, :], ALPHA, None, ALU.mult))
                dve.sem_inc(sums_used, 1)
                with dve.Fori(0, STEPS) as k:
                    chain.enter(k, 3 * SG + SG)
                    with dve.Fori(0, SG - 1) as g:
                        chain.enter(g, 3)
                        finish(k * SG + g, g)
                        chain.leave(SG - 1)
                    m = k * SG + SG - 1
                    for c in range(SG):
                        if c < SG - 1:
                            dve.wait_ge(slot_free, m * (SG - 1) + (SG - 1) + c + 1)
                        else:
                            finish(m, SG - 1)
                        split(c)
                    chain.leave(STEPS)
                dve.wait_ge(z_ready, (STEPS + 1) * SG)
                then(V.tensor_tensor(blocks(acc), blocks(acc), by_node(f2), ALU.mult))
                V.tensor_tensor(xs[:, :], xs[:, :], acc[:, :], ALU.add).then_inc(y_ready, 1)
            with dve.Else():
                chain = Count(general_step)
                then(V.tensor_tensor(blocks(tab), blocks(h), by_node(w_col), ALU.mult))
                then(V.tensor_scalar(h[:, :], h[:, :], ALPHA, None, ALU.mult))
                then(V.tensor_scalar(w_row, w_row, BETA, None, ALU.mult))
                dve.sem_inc(table_ready, 1)
                dve.wait_ge(by_src_in, 16)
                with dve.Fori(0, STEPS) as k:
                    chain.enter(k, 3)
                    sum_edges(L3_FIRST + k * ROUNDS, lambda t: by_src[:, bass.ds(t, GT), 1].bitcast(F32))
                    then(V.tensor_tensor(blocks(acc), blocks(acc), by_node(w_row), ALU.mult))
                    then(V.tensor_tensor(acc[:, :], acc[:, :], h[:, :], ALU.add))
                    then(V.tensor_tensor(blocks(tab), blocks(acc), by_node(w_col), ALU.mult))
                    dve.sem_inc(table_ready, 1)
                    chain.leave(STEPS)
                then(V.tensor_scalar(acc[:, :], acc[:, :], 1.0 / THETA, None, ALU.mult))
                V.tensor_tensor(xs[:, :], xs[:, :], acc[:, :], ALU.add).then_inc(y_ready, 1)


_INS = ["x", "src", "dst", "edge_attr_32", "edge_type_8", "L0_gnn_We", "L0_gnn_be", "L0_gnn_W1", "L0_gnn_b1",
        "L0_gnn_W2", "L0_gnn_b2", "L0_gnn_gamma", "L0_gnn_beta", "L1_gnn_t_emb", "L1_gnn_W1", "L1_gnn_b1",
        "L1_gnn_W2", "L1_gnn_b2", "L1_gnn_We", "L1_gnn_be", "L2_gnn_weights", "L2_gnn_loop_w", "L2_gnn_bias"]

def kernel(**inputs):
    import numpy as _np
    import concourse.bacc as _bacc
    from concourse import mybir as _mybir
    from concourse.bass_utils import run_bass_kernel_spmd as _run

    nc = _bacc.Bacc("TRN2", target_bir_lowering=False, num_devices=1)
    arrays, args = {}, []
    for name in _INS:
        a = _np.ascontiguousarray(inputs[name])
        arrays[f"in_{name}"] = a
        args.append(nc.dram_tensor(f"in_{name}", a.shape, _mybir.dt.from_np(a.dtype), kind="ExternalInput").ap())
    args.append(nc.dram_tensor("out_x", (N, D), _mybir.dt.float32, kind="ExternalOutput").ap())
    build(nc, *args)
    r = _run(nc, [arrays], core_ids=[0])
    return r.results[0]["out_x"]
```
